# Optimizing a Trainium2 kernel written in Bass

```python
import numpy as np
import jax
import jax.numpy as jnp

def _softmax(x, axis=-1):
    return jax.nn.softmax(x, axis=axis)

def _gelu(x):
    return jax.nn.gelu(x, approximate=True)

def _silu(x):
    return jax.nn.silu(x)

def _sigmoid(x):
    return jax.nn.sigmoid(x)

def _layernorm(x, axis=-1, eps=1e-05):
    m = jnp.mean(x, axis=axis, keepdims=True)
    v = jnp.var(x, axis=axis, keepdims=True)
    return (x - m) / jnp.sqrt(v + eps)

def _scatter_add(tgt, idx, src, axis=0):
    return tgt.at[idx].add(src)

def _segment_sum(src, seg, n):
    return jax.ops.segment_sum(src, seg, n)
kernel_name = 'mk_cond_resid_d4_seqx_r4_d2e8c6'

def setup_inputs(seed: int=0):
    np.random.seed(seed)
    _w = jnp.asarray

    def _rec_inputs():
        import jax
        import jax.numpy as jnp
        _rk = jax.random.key(seed)
        x = -7.109e-05 + 0.9999 * jax.random.normal(jax.random.fold_in(_rk, 1), (64, 64, 1024), jnp.float32)
        _lenS = 64 - jax.random.randint(jax.random.fold_in(_rk, 7), (64,), 0, max(1, 64 // 4) + 1, jnp.int32)
        _lenS2 = 64 - jax.random.randint(jax.random.fold_in(_rk, 8), (64,), 0, max(1, 64 // 4) + 1, jnp.int32)
        itok_B_0_15 = jax.random.randint(jax.random.fold_in(_rk, 11), (64,), 0, 16, jnp.int32)
        itok_B_0_2 = jax.random.randint(jax.random.fold_in(_rk, 12), (64,), 0, 3, jnp.int32)
        itok_B_0_7 = jax.random.randint(jax.random.fold_in(_rk, 13), (64,), 0, 8, jnp.int32)
        return (x, itok_B_0_15, itok_B_0_2, itok_B_0_7)
    x, itok_B_0_15, itok_B_0_2, itok_B_0_7 = _rec_inputs()

    def _L0_cond_setup():
        import jax, jax.numpy as jnp
        import numpy as np
        B, C, T = (64, 64, 1024)
        S, D = (16, 64)
        key = jax.random.key(seed)
        k1, k2, k3 = jax.random.split(key, 3)
        x = jax.random.normal(k1, (B, C, T), dtype=jnp.float32)
        condition = jax.random.randint(k2, (B,), 0, S, dtype=jnp.int64)
        bound = float(np.sqrt(6.0 / C))
        weights = jax.random.uniform(k3, (S, C, D), dtype=jnp.float32, minval=-bound, maxval=bound)
        return {'x': x, 'condition': condition, 'weights': weights}
    _L0_cond_all = _L0_cond_setup()
    _L0_cond_in = {k: v for k, v in _L0_cond_all.items() if k in ('weights',)}
    del _L0_cond_all

    def _L1_cond_setup():
        import jax, jax.numpy as jnp
        import numpy as np
        B, S, D_IN, D_OUT = (4, 512, 1024, 1024)
        R, NUM_LABELERS = (32, 5)
        LORA_SCALING = 16 / 32
        key = jax.random.key(seed)
        k1, k2, k3, k4, k5 = jax.random.split(key, 5)
        x = jax.random.normal(k1, (B, S, D_IN), dtype=jnp.float32)
        labeler_index = jax.random.randint(k2, (B,), 0, NUM_LABELERS, dtype=jnp.int64)
        W = jax.random.normal(k3, (D_OUT, D_IN), dtype=jnp.float32) * 0.02
        lora_A = jax.random.normal(k4, (NUM_LABELERS, D_IN, R), dtype=jnp.float32) * 0.02
        lora_B_w = jax.random.normal(k5, (D_OUT, R), dtype=jnp.float32) * 0.02
        return {'x': x, 'labeler_index': labeler_index, 'W': W, 'lora_A': lora_A, 'lora_B_w': lora_B_w}
    _L1_cond_all = _L1_cond_setup()
    _L1_cond_in = {k: v for k, v in _L1_cond_all.items() if k in ('W', 'lora_A', 'lora_B_w')}
    del _L1_cond_all

    def _L2_cond_setup():
        import jax, jax.numpy as jnp
        import numpy as np
        MAX_LORAS = 16
        IN, OUT = (1024, 1024)
        B, S = (8, 512)
        key = jax.random.key(seed)
        k1, k2, k3 = jax.random.split(key, 3)
        x = jax.random.normal(k1, (B, S, IN), dtype=jnp.float32)
        adapter_ids = jax.random.randint(k2, (B,), 0, MAX_LORAS)
        weight = jax.random.normal(k3, (MAX_LORAS, OUT, IN), dtype=jnp.float32) * 0.02
        return {'x': x, 'adapter_ids': adapter_ids, 'weight': weight}
    _L2_cond_all = _L2_cond_setup()
    _L2_cond_in = {k: v for k, v in _L2_cond_all.items() if k in ('weight',)}
    del _L2_cond_all

    def _L3_cond_setup():
        import jax, jax.numpy as jnp
        import numpy as np
        TOP_K = 2
        LANG_BIAS = 5.0
        SCALING = 32.0 / 16.0
        LANGUAGE_PAD_ID = -1
        key = jax.random.key(seed)
        ks = jax.random.split(key, 6)
        B, T, D, O, E, R = (4, 512, 1024, 1024, 8, 16)
        x = jax.random.normal(ks[0], (B, T, D), dtype=jnp.float32)
        language_ids = jax.random.randint(ks[1], (B,), 0, E).astype(jnp.int64)
        W = jax.random.normal(ks[2], (O, D), dtype=jnp.float32) * (1.0 / np.sqrt(D))
        Wr = jax.random.normal(ks[3], (E, D), dtype=jnp.float32) * (1.0 / np.sqrt(D))
        A = jax.random.normal(ks[4], (E, R, D), dtype=jnp.float32) * (1.0 / np.sqrt(D))
        Bm = jax.random.normal(ks[5], (O, R), dtype=jnp.float32) * 0.0
        Bm = jnp.broadcast_to(Bm, (E, O, R)) + jax.random.normal(ks[5], (E, O, R), dtype=jnp.float32) * 0.02
        return {'x': x, 'language_ids': language_ids, 'W': W, 'Wr': Wr, 'A': A, 'B': Bm}
    _L3_cond_all = _L3_cond_setup()
    _L3_cond_in = {k: v for k, v in _L3_cond_all.items() if k in ('W', 'Wr', 'A', 'B')}
    del _L3_cond_all
    return {'x': x, 'itok_B_0_15': itok_B_0_15, 'itok_B_0_2': itok_B_0_2, 'itok_B_0_7': itok_B_0_7, 'L0_cond_weights': _L0_cond_in['weights'], 'L1_cond_W': _L1_cond_in['W'], 'L1_cond_lora_A': _L1_cond_in['lora_A'], 'L1_cond_lora_B_w': _L1_cond_in['lora_B_w'], 'L2_cond_weight': _L2_cond_in['weight'], 'L3_cond_W': _L3_cond_in['W'], 'L3_cond_Wr': _L3_cond_in['Wr'], 'L3_cond_A': _L3_cond_in['A'], 'L3_cond_B': _L3_cond_in['B']}

def reference(x, itok_B_0_15, itok_B_0_2, itok_B_0_7, L0_cond_weights, L1_cond_W, L1_cond_lora_A, L1_cond_lora_B_w, L2_cond_weight, L3_cond_W, L3_cond_Wr, L3_cond_A, L3_cond_B):
    import jax
    import jax.numpy as jnp

    def _L0_cond_ref(x, condition, weights):
        import jax, jax.numpy as jnp
        import numpy as np
        B, C, T = (64, 64, 1024)
        S, D = (16, 64)
        W = weights[condition]
        return jnp.einsum('bct,bcd->bdt', x, W)

    def _L1_cond_ref(x, labeler_index, W, lora_A, lora_B_w):
        import jax, jax.numpy as jnp
        import numpy as np
        B, S, D_IN, D_OUT = (4, 512, 1024, 1024)
        R, NUM_LABELERS = (32, 5)
        LORA_SCALING = 16 / 32
        base = jnp.einsum('bsi,oi->bso', x, W)
        labelers_A = lora_A[labeler_index]
        low = jnp.einsum('bsi,bir->bsr', x, labelers_A)
        delta = jnp.einsum('bsr,or->bso', low, lora_B_w) * LORA_SCALING
        return base + delta

    def _L2_cond_ref(x, adapter_ids, weight):
        import jax, jax.numpy as jnp
        import numpy as np
        MAX_LORAS = 16
        IN, OUT = (1024, 1024)
        B, S = (8, 512)
        w = weight[adapter_ids]
        return jnp.einsum('bsi,boi->bso', x, w)

    def _L3_cond_ref(x, language_ids, W, Wr, A, B):
        import jax, jax.numpy as jnp
        import numpy as np
        TOP_K = 2
        LANG_BIAS = 5.0
        SCALING = 32.0 / 16.0
        LANGUAGE_PAD_ID = -1
        base = jnp.einsum('btd,od->bto', x, W)
        E = Wr.shape[0]
        logits = jnp.einsum('btd,ed->bte', x.astype(jnp.float32), Wr.astype(jnp.float32))
        expert_targets = language_ids
        valid = expert_targets >= 0
        tgt = jnp.where(valid, expert_targets, 0)
        bias = jax.nn.one_hot(tgt, E, dtype=logits.dtype) * LANG_BIAS
        bias = jnp.where(valid[:, None], bias, 0.0)
        logits = logits + bias[:, None, :]
        topw, topi = jax.lax.top_k(logits, TOP_K)
        weights = jax.nn.softmax(topw, axis=-1)
        gates = jnp.sum(jax.nn.one_hot(topi, E, dtype=weights.dtype) * weights[..., None], axis=-2)
        gates = gates.astype(x.dtype)
        h = jnp.einsum('btd,erd->bter', x, A)
        lora_out = jnp.einsum('bter,bte,eor->bto', h, gates, B)
        return base + SCALING * lora_out
    x = x + _L0_cond_ref(x, itok_B_0_15, L0_cond_weights)
    x = x + _L1_cond_ref(x, itok_B_0_2, L1_cond_W, L1_cond_lora_A, L1_cond_lora_B_w)
    x = x + _L2_cond_ref(x, itok_B_0_15, L2_cond_weight)
    x = x + _L3_cond_ref(x, itok_B_0_7, L3_cond_W, L3_cond_Wr, L3_cond_A, L3_cond_B)
    return x

_drawn_inputs = setup_inputs


def setup_inputs(seed=0):
    import zlib

    import numpy as np

    out = dict(_drawn_inputs(seed))
    spreads = {}
    factors = {}
    for name, (base, spread) in spreads.items():
        noise = np.random.default_rng([zlib.crc32(name.encode()), seed]).standard_normal(out[name].shape)
        drawn = base * np.exp(spread * noise) if base else spread * noise
        out[name] = jnp.asarray(drawn.astype(out[name].dtype))
    for name, factor in factors.items():
        out[name] = (out[name] * factor).astype(out[name].dtype)
    return out
```

```python
from contextlib import ExitStack

import concourse.bass as bass
from concourse import mybir

ALU = mybir.AluOpType
ACT = mybir.ActivationFunctionType
F32 = mybir.dt.float32
F32R = mybir.dt.float32r
F16 = mybir.dt.float16
I32 = mybir.dt.int32
U32 = mybir.dt.uint32
X = mybir.AxisListType.X
ABSMAX = bass.bass_isa.ReduceOp.absmax

P = 128
EXPONENT = 0x7F800000
HI, LO = 0, 1
PASSES = [(HI, HI), (HI, LO), (LO, HI)]
TOP = 14
SCALE_MAX = 2.0 ** 60
WCHUNK = 2048


def cond_stack_kernel(nc, x, ids, W0, W1, A1, B1, W2, W3, A3, B3, shape_consts, out):
    B, C, D = x.shape
    NT = B * C // P
    K = D // P
    R1 = B1.shape[0]
    NL = A1.shape[2] // R1
    N1 = A1.shape[2]
    NE = A3.shape[2] - P
    N3 = A3.shape[2]
    RE = P // NE
    WN = K * D
    BANK = 512
    HALVES = D // BANK
    assert 2 * C == P and NT * 2 == B

    with ExitStack() as ctx:
        def sb(name, shape, dt):
            return ctx.enter_context(nc.sbuf_tensor(name, shape, dt))

        def ps(name, shape, dt):
            return ctx.enter_context(nc.psum_tensor(name, shape, dt))

        def sem(name):
            return ctx.enter_context(nc.semaphore(name))

        w1 = sb("w1", [P, 2, WN], F16)
        w3 = sb("w3", [P, 2, WN], F16)
        w2 = sb("w2", [P, 2 * 2 * WN], F16)
        raw = sb("raw", [P, WN], F32)
        a1 = sb("a1", [P, 2, K * N1], F16)
        a3 = sb("a3", [P, 2, K * N3], F16)
        b1 = sb("b1", [3 * R1, D], F32R)
        b3 = sb("b3", [P, 2, D], F32R)
        w0 = sb("w0", [P, P], F32)
        xs = sb("xs", [P, 4, D], F32)
        xin, x1, x2, x3 = (xs[:, i, :] for i in range(4))
        parts = sb("parts", [P, 2, D], F16)
        xT = [sb(f"x{n}T", [P, 2, K, P], F16) for n in (1, 2, 3)]
        identh = sb("identh", [P, P], F16)
        consts = sb("consts", [P, P + B + 1], F32)
        ident, iotar, iotac = consts[:, 0:P], consts[0:B, P:P + B], consts[0:B, P + B:P + B + 1]
        iotae = consts[:, P:P + NE]
        ones = sb("ones", [1, P], F32)
        rowmax = sb("rowmax", [P, 3], F32)
        expo = sb("expo", [P, 3], F32)
        flip = sb("flip", [P, 3], F32)
        scale = sb("scale", [P, 3], F32)
        unscale = sb("unscale", [P, 3], F32)
        inv3 = sb("inv3", [P, 1], F32)
        NW = 6
        W1_, A1_, W3_, A3_, SLOT = 0, 1, 2, 3, 4
        partmax = sb("partmax", [P, WN // WCHUNK], F32)
        wmax = sb("wmax", [P, 2], F32)
        wall = sb("wall", [P, 1], F32)
        onecol = sb("onecol", [P, 1], F32)
        wexpo = sb("wexpo", [P, 1], F32)
        wflip = sb("wflip", [P, 1], F32)
        wscale = sb("wscale", [P, NW], F32)
        winv = sb("winv", [P, NW], F32)
        winvtop = sb("winvtop", [P, NW], F32)
        c1 = sb("c1", [P, 1], F32)
        c3 = sb("c3", [P, 1], F32)
        w2inv = sb("w2inv", [P, 3], F32)
        lowm = sb("lowm", [P, R1, NL], F32)
        low = sb("low", [P, R1], F32)
        lowp = sb("lowp", [P, 3, R1], F32R)
        lowT = sb("lowT", [3 * R1, P], F32R)
        logits = sb("logits", [P, NE], F32)
        top8 = sb("top8", [P, 8], F32)
        topi = sb("topi", [P, 8], U32)
        topf = sb("topf", [P, 8], F32)
        nmax = sb("nmax", [P, 1], F32)
        g = sb("g", [P, 4], F32)
        gates = sb("gates", [P, 2, NE], F32)
        hg = sb("hg", [P, P], F32)
        hgp = sb("hgp", [P, 2, P], F32R)
        hgT = sb("hgT", [P, 2, P], F32R)
        scratch = parts[:, :, :].rearrange("p a n -> p (a n)").bitcast(F32)
        scratch_end = [0]

        def in_parts(rows, cols, dt=F32):
            at, scratch_end[0] = scratch_end[0], scratch_end[0] + cols
            assert scratch_end[0] <= D
            return scratch[0:rows, at:at + cols].bitcast(dt)

        vals = sb("vals", [B, 4], F32)
        keycol = sb("keycol", [B, 1], F32)
        pos = sb("pos", [B, 1], F32)
        keyrow = in_parts(B, B)
        idrow = in_parts(B, B, I32)
        idrowf = in_parts(B, B)
        idcol = sb("idcol", [B, 3], I32)
        before = in_parts(B, B)
        perm1h = in_parts(B, B)
        srt = in_parts(1, 4 * B).rearrange("p (n b) -> p n b", n=4)
        new = in_parts(1, B)
        zrow = in_parts(1, B)
        rank = in_parts(1, B)
        parity = in_parts(1, B)
        VARIANT, N_1, N_2, R_1, R_2, AD_1, AD_2, SL_1, SL_2, NCTL = range(10)
        ctlf = raw[0:1, 0:NCTL * (NT + 1)].rearrange("p (n t) -> p n t", n=NCTL)
        ctl = sb("ctl", [1, NCTL, NT + 1], I32)
        batch = sb("batch", [1, B], I32)
        tok = sb("tok", [P, 3, NT], F32)
        notslot = sb("notslot", [P, NT], F32)
        lmask = sb("lmask", [P, NT, NL], F32)
        lbias = sb("lbias", [P, NE], F32)

        w0id = sb("w0id", [1, B], I32)
        a1raw = xs[:, 1:4, :].rearrange("p a d -> p (a d)")[:, 0:K * N1]
        a3raw = xs[:, 1:4, :].rearrange("p a d -> p (a d)")[:, K * N1:K * (N1 + N3)]
        w1raw = w2[:, 2 * WN:4 * WN].bitcast(F32)
        b1raw = xT[2][0:3 * R1].rearrange("p a k n -> p (a k n)").bitcast(F32)
        b3raw = xT[1][:, :, :, :].rearrange("p a k n -> p (a k n)").bitcast(F32)

        psY = ps("psY", [P, D], F32)
        psZ = ps("psZ", [P, D], F32)
        psT = ps("psT", [P, 2, K, P], F16)
        psS = ps("psS", [P, BANK], F32)
        psU = ps("psU", [P, BANK], F32)

        ids_loaded = sem("ids_loaded")
        b1_loaded, b3_loaded = sem("b1_loaded"), sem("b3_loaded")
        a_loaded = [sem("a1_loaded"), sem("a3_loaded")]
        w1_loaded = [sem(f"w1_loaded{c}") for c in range(WN // WCHUNK)]
        raw_loaded = [sem(f"raw_loaded{c}") for c in range(WN // WCHUNK)]
        x_loaded = sem("x_loaded")
        w0_loaded = sem("w0_loaded")
        stored = sem("stored")
        keys_ready = sem("keys_ready")
        sorted_done = sem("sorted_done")
        ctl_ready = sem("ctl_ready")
        tok_done = sem("tok_done")
        route_chain = sem("route_chain")
        wmax_ready = sem("wmax_ready")
        wall_ready = sem("wall_ready")
        wscale_ready = sem("wscale_ready")
        partmax_ready = sem("partmax_ready")
        fixed_hi, fixed_lo = sem("fixed_hi"), sem("fixed_lo")
        b_chain = sem("b_chain")
        b1_ready, b3_ready = sem("b1_ready"), sem("b3_ready")
        whi_ready = sem("whi_ready")
        wlo_ready = sem("wlo_ready")
        wprep_chain = sem("wprep_chain")
        tile_whi = sem("tile_whi")
        tile_wlo = sem("tile_wlo")
        l0_done, l1_done, l2_done, l3_done = (sem(f"l{n}_done") for n in range(4))
        la1_done, la3_done = sem("la1_done"), sem("la3_done")
        xT_done = [sem(f"x{n}T_done") for n in (1, 2, 3)]
        lowT_done, hgT_done = sem("lowT_done"), sem("hgT_done")
        x_ready = [sem(f"x{n}_ready") for n in (1, 2, 3)]
        scale_ready = [sem(f"scale{n}_ready") for n in (1, 2, 3)]
        lo_ready = [sem(f"lo{n}_ready") for n in (1, 2, 3)]
        hi_ready = [sem(f"hi{n}_ready") for n in (1, 2, 3)]
        xT_copied = [sem(f"x{n}T_copied") for n in (1, 2, 3)]
        low_masked, low_ready, lowT_copied = sem("low_masked"), sem("low_ready"), sem("lowT_copied")
        top_ready, exp_ready, hg_ready, hgT_copied = (
            sem(n) for n in ("top_ready", "exp_ready", "hg_ready", "hgT_copied"))
        out_ready = sem("out_ready")
        scale_chain = [sem(f"scale{n}_chain") for n in (1, 2, 3)]
        gate_chain = sem("gate_chain")
        hg_chain = sem("hg_chain")
        low_chain = sem("low_chain")

        NCHUNK = WN // WCHUNK
        AT_A1, AT_A3, AT_W1 = 0, 1, 2

        def at_adapter(prior, later):
            return prior + (4 if later else 3)

        def at_w3(prior):
            return prior + 3

        def split_before(prior):
            return prior * NCHUNK + NCHUNK

        def raw_before(prior, later):
            return prior + 1 if later else prior

        SMALL_CHUNKS = 2

        block = ctx.enter_context(nc.Block())

        @block.sync
        def _(sp):
            def load_x(u, batch_of):
                if not (isinstance(u, int) and u == 0):
                    sp.wait_ge(x_ready[0], u)
                for h in range(2):
                    b = batch_of(h)
                    rows = slice(h * C, h * C + C)
                    sp.dma_start(xin[rows, :], x[bass.ds(b, 1)].rearrange("b c d -> (b c) d")
                                 ).then_inc(x_loaded, 16)

            def load_w0(u, adapter_of):
                for h in range(2):
                    rows = slice(h * C, h * C + C)
                    sp.dma_start(w0[rows, rows], W0[bass.ds(adapter_of(h), 1)].rearrange("a c d -> (a c) d")
                                 ).then_inc(w0_loaded, 16)

            def tile_loads(u):
                load_x(u, lambda h: sp.value_load(batch[0:1, bass.ds(2 * u + h, 1)], min_val=0, max_val=B - 1))
                load_w0(u, lambda h: sp.value_load(w0id[0:1, bass.ds(2 * u + h, 1)], min_val=0, max_val=W2.shape[0] - 1))

            def load_adapter(u, which, later=True):
                flag, r, ad = ((N_1, R_1, AD_1), (N_2, R_2, AD_2))[which]
                n = sp.value_load(ctl[0:1, flag, bass.ds(u, 1)], min_val=0, max_val=1)
                prior = sp.value_load(ctl[0:1, r, bass.ds(u, 1)], min_val=0, max_val=W2.shape[0] - 1)
                a = sp.value_load(ctl[0:1, ad, bass.ds(u, 1)], min_val=0, max_val=W2.shape[0] - 1)
                with sp.If(n > 0):
                    for c in range(NCHUNK):
                        cols = slice(c * WCHUNK, c * WCHUNK + WCHUNK)
                        if later or which:
                            sp.wait_ge(whi_ready, split_before(prior) - NCHUNK + c + 1)
                            sp.wait_ge(wlo_ready, split_before(prior) - NCHUNK + c + 1)
                        sp.dma_start(raw[:, cols], W2[bass.ds(a, 1)].rearrange("a p n -> (a p) n")[:, cols]
                                     ).then_inc(raw_loaded[c], 16)

            def load_w3():
                prior = sp.value_load(ctl[0:1, R_2, 0:1], min_val=0, max_val=1)
                for c in range(NCHUNK):
                    cols = slice(c * WCHUNK, c * WCHUNK + WCHUNK)
                    sp.wait_ge(whi_ready, split_before(prior) + c + 1)
                    sp.wait_ge(wlo_ready, split_before(prior) + c + 1)
                    sp.dma_start(raw[:, cols], W3[:, cols]).then_inc(raw_loaded[c], 16)

            def store(u):
                sp.wait_ge(out_ready, u + 1)
                for h in range(2):
                    b = sp.value_load(batch[0:1, bass.ds(2 * u + h, 1)], min_val=0, max_val=B - 1)
                    sp.dma_start(out[bass.ds(b, 1)].rearrange("b c d -> (b c) d"), x3[h * C:h * C + C, :]
                                 ).then_inc(stored, 16)

            for n in range(3):
                sp.dma_start(idcol[:, n:n + 1], ids[n].rearrange("(b o) -> b o", o=1)).then_inc(ids_loaded, 16)
            sp.dma_start(idrow[:, :], ids[0].partition_broadcast(B)).then_inc(ids_loaded, 16)
            sp.dma_start(consts[:, :], shape_consts).then_inc(ids_loaded, 16)
            sp.dma_start(a1raw, A1.rearrange("p k n -> p (k n)")).then_inc(a_loaded[0], 16)
            sp.dma_start(a3raw, A3.rearrange("p k n -> p (k n)")).then_inc(a_loaded[1], 16)
            for c in range(NCHUNK):
                cols = slice(c * WCHUNK, c * WCHUNK + WCHUNK)
                sp.dma_start(w1raw[:, cols], W1[:, cols]).then_inc(w1_loaded[c], 16)
            sp.wait_ge(ctl_ready, 1)
            tile_loads(0)
            load_adapter(0, 0, later=False)
            for i in range(3):
                sp.dma_start(b1raw[i * R1:i * R1 + R1, :], B1).then_inc(b1_loaded, 16)
            sp.dma_start(b3raw, B3).then_inc(b3_loaded, 16)
            load_adapter(0, 1, later=False)
            tile_loads(1)
            load_w3()
            sp.wait_ge(fixed_hi, SMALL_CHUNKS + NCHUNK)
            sp.wait_ge(fixed_lo, SMALL_CHUNKS + NCHUNK)
            load_adapter(1, 0)
            load_adapter(1, 1)
            with sp.Fori(1, NT - 1) as t:
                tile_loads(t + 1)
                load_adapter(t + 1, 0)
                store(t - 1)
                load_adapter(t + 1, 1)
            store(NT - 2)
            store(NT - 1)
            sp.wait_ge(stored, 32 * NT)


        @block.gpsimd
        def _(pool):
            def over_partitions(c):
                pool.wait_ge(wmax_ready, c + 1)
                nc.gpsimd.tensor_tensor(wmax[:, 1:2], wmax[:, 0:1], onecol[:, :], ALU.mult)
                pool.drain()
                nc.gpsimd.partition_all_reduce(wall[:, 0:1], wmax[:, 1:2], P, ABSMAX).then_inc(wall_ready, 1)

            nc.gpsimd.memset(onecol[:, :], 1.0)
            pool.drain()
            def new_adapters(u, later):
                for which in range(2):
                    flag, r = ((N_1, R_1), (N_2, R_2))[which]
                    n = pool.value_load(ctl[0:1, flag, bass.ds(u, 1)], min_val=0, max_val=1)
                    prior = pool.value_load(ctl[0:1, r, bass.ds(u, 1)], min_val=0, max_val=NT)
                    with pool.If(n > 0):
                        over_partitions(at_adapter(prior, later))

            over_partitions(AT_A1)
            over_partitions(AT_A3)
            over_partitions(AT_W1)
            pool.wait_ge(ctl_ready, 1)
            new_adapters(0, False)
            over_partitions(at_w3(pool.value_load(ctl[0:1, R_2, 0:1], min_val=0, max_val=1) + 1))
            with pool.Fori(1, NT) as t:
                new_adapters(t, True)

        @block.scalar
        def _(act):
            def high_parts(chunks, src, dst, n, scale_ap, done):
                for c in chunks:
                    at, m = c * WCHUNK, min(n, c * WCHUNK + WCHUNK)
                    nc.scalar.activation(dst(at, m), src[:, at:m], ACT.Copy, scale=scale_ap).then_inc(done, 1)

            def new_adapter(u, which, chunks, later):
                flag, r, sl = ((N_1, R_1, SL_1), (N_2, R_2, SL_2))[which]
                n = act.value_load(ctl[0:1, flag, bass.ds(u, 1)], min_val=0, max_val=1)
                prior = act.value_load(ctl[0:1, r, bass.ds(u, 1)], min_val=0, max_val=NT)
                slot = act.value_load(ctl[0:1, sl, bass.ds(u, 1)], min_val=0, max_val=1)
                with act.If(n > 0):
                    act.wait_ge(wscale_ready, at_adapter(prior, later) + 1)
                    high_parts(chunks, raw, lambda c, m: w2[:, bass.ds(slot * (2 * WN) + c, m - c)], WN,
                               wscale[:, bass.ds(slot + SLOT, 1)], whi_ready)

            def high_part(n, u):
                act.wait_ge(scale_ready[n], u + 1)
                nc.scalar.activation(parts[:, HI, :], (x1, x2, x3)[n], ACT.Copy, scale=scale[:, n:n + 1]
                                     ).then_inc(hi_ready[n], 1)

            def copy_transposed(n, u):
                act.wait_ge(xT_done[n], u + 1)
                nc.scalar.copy(xT[n][:, HI], psT[:, HI])
                nc.scalar.copy(xT[n][:, LO], psT[:, LO]).then_inc(xT_copied[n], 1)

            def copy_lowT(u):
                act.wait_ge(lowT_done, u + 1)
                nc.scalar.copy(lowT[:, :], psU[0:3 * R1, 0:P]).then_inc(lowT_copied, 1)

            def copy_hgT(u):
                act.wait_ge(hgT_done, u + 1)
                nc.scalar.copy(hgT[:, :, :], psU[:, 0:2 * P].rearrange("p (a n) -> p a n", a=2)).then_inc(hgT_copied, 1)

            def gate_exp(u):
                act.wait_ge(top_ready, u + 1)
                nc.scalar.activation(g[:, 0:1], top8[:, 1:2], ACT.Exp, bias=nmax[:, 0:1]).then_inc(exp_ready, 1)

            def tile_step(t, first, last):
                if not first:
                    copy_transposed(2, t - 1)
                    new_adapter(t, 0, [2], True)
                copy_lowT(t)
                if not first:
                    new_adapter(t, 0, [3], True)
                    new_adapter(t, 1, range(NCHUNK), True)
                else:
                    new_adapter(0, 0, range(NCHUNK), False)
                    new_adapter(0, 1, range(NCHUNK), False)
                act.drain().then_inc(tile_whi, 1)
                act.wait_ge(*((xT_done[0], 1) if first else (xT_done[2], t)))
                high_part(1, t)
                if not first:
                    gate_exp(t - 1)
                copy_transposed(1, t)
                if not last:
                    high_part(0, t + 1)
                if not first:
                    copy_hgT(t - 1)
                if not last:
                    copy_transposed(0, t + 1)
                if first:
                    act.wait_ge(wscale_ready, at_w3(act.value_load(ctl[0:1, R_2, 0:1], min_val=0, max_val=1) + 1) + 1)
                    high_parts(range(NCHUNK), raw, lambda c, m: w3[:, HI, c:m], WN, wscale[:, W3_:W3_ + 1], fixed_hi)
                high_part(2, t)
                if not last:
                    new_adapter(t + 1, 0, [0, 1], True)

            act.wait_ge(wscale_ready, AT_A1 + 1)
            high_parts([0], a1raw, lambda c, m: a1[:, HI, c:m], K * N1, wscale[:, A1_:A1_ + 1], fixed_hi)
            act.wait_ge(wscale_ready, AT_A3 + 1)
            high_parts([0], a3raw, lambda c, m: a3[:, HI, c:m], K * N3, wscale[:, A3_:A3_ + 1], fixed_hi)
            act.wait_ge(wscale_ready, AT_W1 + 1)
            high_parts(range(NCHUNK), w1raw, lambda c, m: w1[:, HI, c:m], WN, wscale[:, W1_:W1_ + 1], whi_ready)
            act.wait_ge(ctl_ready, 1)
            high_part(0, 0)
            copy_transposed(0, 0)
            tile_step(0, True, False)
            with act.Fori(1, NT - 1) as t:
                tile_step(t, False, False)
            tile_step(NT - 1, False, True)
            copy_transposed(2, NT - 1)
            gate_exp(NT - 1)
            copy_hgT(NT - 1)

        @block.vector
        def _(dve):
            def scale_from(maxima, e, f, chain, base):
                nc.vector.tensor_scalar(f.bitcast(I32), maxima.bitcast(I32), EXPONENT, EXPONENT,
                                        ALU.bitwise_and, ALU.bitwise_xor).then_inc(chain, 1)
                nc.vector.tensor_scalar(e.bitcast(I32), maxima.bitcast(I32), EXPONENT, None,
                                        ALU.bitwise_and).then_inc(chain, 1)
                dve.wait_ge(chain, base + 2)

            WLINKS = 4

            def weight_scale(i, col, src, n, loaded):
                for c, (semaphore, value) in enumerate(loaded):
                    at, m = c * WCHUNK, min(n, c * WCHUNK + WCHUNK)
                    dve.wait_ge(semaphore, value)
                    last = nc.vector.tensor_reduce(partmax[:, c:c + 1], src[:, at:m], X, ALU.max,
                                                   apply_absolute_value=True)
                last.then_inc(partmax_ready, 1)
                dve.wait_ge(partmax_ready, i + 1)
                nc.vector.tensor_reduce(wmax[:, 0:1], partmax[:, 0:len(loaded)], X, ALU.max).then_inc(wmax_ready, 1)
                dve.wait_ge(wall_ready, i + 1)
                base = i * WLINKS
                scale_from(wall[:, 0:1], wexpo[:, :], wflip[:, :], wprep_chain, base)
                at = bass.ds(col, 1)
                nc.vector.tensor_scalar(winv[:, at], wexpo[:, :], 2.0 ** TOP / SCALE_MAX, 2.0 ** -TOP,
                                        ALU.max, ALU.mult).then_inc(wprep_chain, 1)
                nc.vector.tensor_scalar(winvtop[:, at], wexpo[:, :], 2.0 ** TOP / SCALE_MAX, 2.0 ** (-2 * TOP),
                                        ALU.max, ALU.mult).then_inc(wprep_chain, 1)
                nc.vector.tensor_scalar(wscale[:, at], wflip[:, :], 2.0 ** (TOP - 1), SCALE_MAX,
                                        ALU.mult, ALU.min).then_inc(wscale_ready, 1)

            def low_parts(i, src, hi, lo, n, scale_ap, hi_done, hi_base, lo_done):
                dve.wait_ge(wprep_chain, i * WLINKS + WLINKS)
                dve.wait_ge(wscale_ready, i + 1)
                for j, c in enumerate(range(0, n, WCHUNK)):
                    m = min(n, c + WCHUNK)
                    dve.wait_ge(hi_done, hi_base + j + 1)
                    nc.vector.scalar_tensor_tensor(out=lo(c, m), in0=src[:, c:m], scalar=scale_ap, in1=hi(c, m),
                                                   op0=ALU.mult, op1=ALU.subtract).then_inc(lo_done, 1)

            def raw_chunks(before):
                return [(semaphore, before * 16 + 16) for semaphore in raw_loaded]

            def adapter_event(u, which, body, later=True):
                flag, r, sl = ((N_1, R_1, SL_1), (N_2, R_2, SL_2))[which]
                n = dve.value_load(ctl[0:1, flag, bass.ds(u, 1)], min_val=0, max_val=1)
                prior = dve.value_load(ctl[0:1, r, bass.ds(u, 1)], min_val=0, max_val=NT)
                slot = dve.value_load(ctl[0:1, sl, bass.ds(u, 1)], min_val=0, max_val=1)
                with dve.If(n > 0):
                    body(prior, slot, later)

            def adapter_scale(prior, slot, later):
                weight_scale(at_adapter(prior, later), slot + SLOT, raw, WN, raw_chunks(raw_before(prior, later)))

            def adapter_low(prior, slot, later):
                low_parts(at_adapter(prior, later), raw, lambda c, m: w2[:, bass.ds(slot * (2 * WN) + c, m - c)],
                          lambda c, m: w2[:, bass.ds(slot * (2 * WN) + (WN + c), m - c)], WN,
                          wscale[:, bass.ds(slot + SLOT, 1)], whi_ready, split_before(prior), wlo_ready)

            def adapter_both(prior, slot, later):
                adapter_scale(prior, slot, later)
                adapter_low(prior, slot, later)

            def new_adapters(u, later=True):
                adapter_event(u, 0, adapter_low, later)
                adapter_event(u, 1, adapter_both, later)
                dve.drain().then_inc(tile_wlo, 1)

            ROWLINKS = (4, 6, 5)

            def split_rows(n, u):
                src = (x1, x2, x3)[n]
                base = u * ROWLINKS[n]
                dve.wait_ge(x_ready[n], u + 1)
                nc.vector.tensor_reduce(rowmax[:, n:n + 1], src, X, ALU.max, apply_absolute_value=True
                                        ).then_inc(scale_chain[n], 1)
                dve.wait_ge(scale_chain[n], base + 1)
                e, f = expo[:, n:n + 1], flip[:, n:n + 1]
                scale_from(rowmax[:, n:n + 1], e, f, scale_chain[n], base + 1)
                nc.vector.tensor_scalar(scale[:, n:n + 1], f, 2.0 ** (TOP - 1), SCALE_MAX,
                                        ALU.mult, ALU.min).then_inc(scale_ready[n], 1)
                if n == 1:
                    nc.vector.tensor_tensor(w2inv[:, 0:1], winvtop[:, SLOT:SLOT + 1], notslot[:, bass.ds(u, 1)],
                                            ALU.mult).then_inc(scale_chain[n], 1)
                    dve.wait_ge(scale_chain[n], base + 4)
                    nc.vector.scalar_tensor_tensor(out=w2inv[:, 1:2], in0=winvtop[:, SLOT + 1:SLOT + 2],
                                                   scalar=tok[:, 2, bass.ds(u, 1)], in1=w2inv[:, 0:1],
                                                   op0=ALU.mult, op1=ALU.add).then_inc(scale_chain[n], 1)
                    dve.wait_ge(scale_chain[n], base + 5)
                by = (winvtop[:, W1_:W1_ + 1], w2inv[:, 1:2], winvtop[:, W3_:W3_ + 1])[n]
                nc.vector.tensor_scalar(unscale[:, n:n + 1], e, 2.0 ** TOP / SCALE_MAX, by,
                                        ALU.max, ALU.mult).then_inc(scale_chain[n], 1)
                if n == 2:
                    nc.vector.tensor_scalar(inv3[:, :], e, 2.0 ** TOP / SCALE_MAX, winvtop[:, A3_:A3_ + 1],
                                            ALU.max, ALU.mult).then_inc(scale_chain[n], 1)
                dve.wait_ge(hi_ready[n], u + 1)
                dve.wait_ge(scale_ready[n], u + 1)
                dve.wait_ge(scale_chain[n], base + ROWLINKS[n])
                nc.vector.scalar_tensor_tensor(out=parts[:, LO, :], in0=src, scalar=scale[:, n:n + 1],
                                               in1=parts[:, HI, :], op0=ALU.mult, op1=ALU.subtract
                                               ).then_inc(lo_ready[n], 1)

            def make_x1(u):
                dve.wait_ge(l0_done, u + 1)
                nc.vector.tensor_tensor(x1, psZ[:, :], xin, ALU.add).then_inc(x_ready[0], 1)
                split_rows(0, u)

            def make_x2(u):
                dve.wait_ge(l1_done, u + 1)
                nc.vector.scalar_tensor_tensor(out=x2, in0=psY[:, :], scalar=unscale[:, 0:1], in1=x1,
                                               op0=ALU.mult, op1=ALU.add).then_inc(x_ready[1], 1)
                split_rows(1, u)

            def make_x3(u, first):
                dve.wait_ge(l2_done, u + 1)
                if not first:
                    dve.wait_ge(stored, u * 32)
                nc.vector.scalar_tensor_tensor(out=x3, in0=psZ[:, :], scalar=unscale[:, 1:2], in1=x2,
                                               op0=ALU.mult, op1=ALU.add).then_inc(x_ready[2], 1)
                split_rows(2, u)

            def make_out(u):
                dve.wait_ge(l3_done, u + 1)
                nc.vector.scalar_tensor_tensor(out=x3, in0=psY[:, :], scalar=unscale[:, 2:3], in1=x3,
                                               op0=ALU.mult, op1=ALU.add).then_inc(out_ready, 1)

            def make_low(u):
                dve.wait_ge(la1_done, u + 1)
                nc.vector.scalar_tensor_tensor(
                    out=lowm[:, :, :], in0=psS[:, 0:N1].rearrange("p (l r) -> p r l", l=NL), scalar=c1[:, 0:1],
                    in1=lmask[:, bass.ds(u, 1), :].to_broadcast([P, R1, NL]),
                    op0=ALU.mult, op1=ALU.mult).then_inc(low_masked, 1)
                dve.wait_ge(low_masked, u + 1)
                nc.vector.tensor_reduce(low[:, :], lowm[:, :, :], X, ALU.add).then_inc(low_chain, 1)
                dve.wait_ge(low_chain, u * 2 + 1)
                nc.vector.tensor_copy(lowp[:, 2, :], low[:, :])
                nc.vector.tensor_copy(lowp[:, 0, :], low[:, :]).then_inc(low_chain, 1)
                dve.wait_ge(low_chain, u * 2 + 2)
                nc.vector.tensor_tensor(lowp[:, 1, :], low[:, :], lowp[:, 0, :].bitcast(F32), ALU.subtract
                                        ).then_inc(low_ready, 1)

            GLINKS = 11

            def make_gates(u):
                base = u * GLINKS
                nc.vector.tensor_scalar(lbias[:, :], iotae, tok[:, 1, bass.ds(u, 1)], 5.0, ALU.is_equal, ALU.mult
                                        ).then_inc(gate_chain, 1)
                dve.wait_ge(gate_chain, base + 1)
                dve.wait_ge(la3_done, u + 1)
                nc.vector.scalar_tensor_tensor(out=logits[:, :], in0=psS[:, P:N3], scalar=inv3[:, 0:1],
                                               in1=lbias[:, :],
                                               op0=ALU.mult, op1=ALU.add).then_inc(gate_chain, 1)
                dve.drain()
                nc.vector.max(top8[:, :], logits[:, :]).then_inc(gate_chain, 1)
                dve.wait_ge(gate_chain, base + 3)
                nc.vector.tensor_scalar(nmax[:, :], top8[:, 0:1], -1.0, None, ALU.mult).then_inc(top_ready, 1)
                nc.vector.max_index(topi[:, :], top8[:, :], logits[:, :]).then_inc(gate_chain, 1)
                dve.wait_ge(gate_chain, base + 4)
                nc.vector.tensor_copy(topf[:, :], topi[:, :]).then_inc(gate_chain, 1)
                dve.wait_ge(exp_ready, u + 1)
                nc.vector.tensor_scalar(g[:, 1:2], g[:, 0:1], 1.0, None, ALU.add).then_inc(gate_chain, 1)
                dve.wait_ge(gate_chain, base + 6)
                nc.vector.reciprocal(g[:, 2:3], g[:, 1:2]).then_inc(gate_chain, 1)
                dve.wait_ge(gate_chain, base + 7)
                nc.vector.tensor_scalar(g[:, 3:4], g[:, 2:3], g[:, 0:1], c3[:, 0:1], ALU.mult, ALU.mult
                                        ).then_inc(gate_chain, 1)
                nc.vector.tensor_scalar(gates[:, 0, :], iotae, topf[:, 0:1], g[:, 2:3], ALU.is_equal, ALU.mult
                                        ).then_inc(gate_chain, 1)
                dve.wait_ge(gate_chain, base + 9)
                nc.vector.tensor_scalar(gates[:, 1, :], iotae, topf[:, 1:2], g[:, 3:4], ALU.is_equal, ALU.mult
                                        ).then_inc(gate_chain, 1)
                dve.wait_ge(gate_chain, base + 10)
                nc.vector.scalar_tensor_tensor(out=gates[:, 0, :], in0=gates[:, 0, :], scalar=c3[:, 0:1],
                                               in1=gates[:, 1, :], op0=ALU.mult, op1=ALU.add
                                               ).then_inc(gate_chain, 1)
                dve.wait_ge(gate_chain, base + 11)
                nc.vector.tensor_tensor(hg[:, :].rearrange("p (e r) -> p e r", e=NE),
                                        psS[:, 0:P].rearrange("p (e r) -> p e r", e=NE),
                                        gates[:, 0, :].unsqueeze(2).to_broadcast([P, NE, RE]),
                                        ALU.mult).then_inc(hg_chain, 1)
                dve.wait_ge(hg_chain, u * 2 + 1)
                nc.vector.tensor_copy(hgp[:, HI, :], hg[:, :]).then_inc(hg_chain, 1)
                dve.wait_ge(hg_chain, u * 2 + 2)
                nc.vector.tensor_tensor(hgp[:, LO, :], hg[:, :], hgp[:, HI, :].bitcast(F32), ALU.subtract
                                        ).then_inc(hg_ready, 1)

            def tile_step(t, first, last):
                make_x2(t)
                if not first:
                    make_gates(t - 1)
                if not last:
                    make_x1(t + 1)
                if first:
                    prepare_w3()
                if not last:
                    adapter_event(t + 1, 0, adapter_scale)
                if not first:
                    make_out(t - 1)
                make_x3(t, first)
                if not last:
                    make_low(t + 1)
                    new_adapters(t + 1)

            links = [0]

            def link(ins):
                ins.then_inc(route_chain, 1)
                links[0] += 1
                dve.wait_ge(route_chain, links[0])

            nc.vector.memset(ones[:, :], 1.0)
            nc.vector.memset(winvtop[:, :], 1.0)
            nc.vector.memset(zrow[:, :], 0.0)
            nc.vector.memset(new[:, 0:1], 1.0)
            nc.vector.memset(ctlf[:, :, :], 0.0)
            link(nc.vector.memset(w0[:, :], 0.0))
            dve.wait_ge(ids_loaded, 16 * 5)
            nc.vector.tensor_copy(identh[:, :], ident)
            nc.vector.tensor_copy(vals[:, 0:1], iotac)
            nc.vector.tensor_copy(vals[:, 1:4], idcol[:, :])
            link(nc.vector.tensor_copy(idrowf[:, :], idrow[:, :]))
            nc.vector.scalar_tensor_tensor(out=keyrow[:, :], in0=idrowf[:, :], scalar=float(B), in1=iotar,
                                           op0=ALU.mult, op1=ALU.add)
            link(nc.vector.scalar_tensor_tensor(out=keycol[:, :], in0=vals[:, 1:2], scalar=float(B), in1=iotac,
                                                op0=ALU.mult, op1=ALU.add))
            link(nc.vector.tensor_scalar(before[:, :], keyrow[:, :], keycol[:, 0:1], None, ALU.is_lt))
            link(nc.vector.tensor_reduce(pos[:, :], before[:, :], X, ALU.add))
            nc.vector.tensor_scalar(perm1h[:, :], iotar, pos[:, 0:1], None, ALU.is_equal).then_inc(keys_ready, 1)
            dve.wait_ge(sorted_done, 1)
            link(nc.vector.tensor_copy(srt[:, :, :], psS[0:1, 0:4 * B].rearrange("p (n b) -> p n b", n=4)))
            nc.vector.tensor_copy(batch[:, :], srt[:, 0, :])
            nc.vector.tensor_copy(w0id[:, :], srt[:, 1, :])
            link(nc.vector.tensor_tensor(new[:, 1:B], srt[:, 1, 1:B], srt[:, 1, 0:B - 1], ALU.not_equal))
            nc.vector.tensor_tensor_scan(rank[:, :], new[:, :], zrow[:, :], 0.0, ALU.add, ALU.add)
            nc.vector.tensor_tensor_scan(parity[:, :], new[:, :], zrow[:, :], 1.0, ALU.not_equal, ALU.add
                                         ).then_inc(route_chain, 1)
            links[0] += 1
            dve.wait_ge(route_chain, links[0])

            def pair(row, h):
                return row.rearrange("p (t h) -> p h t", h=2)[:, h, :]

            def ctl_row(n):
                return ctlf[:, n, 0:NT]

            new0, new1 = pair(new[:, :], 0), pair(new[:, :], 1)
            par0, par1 = pair(parity[:, :], 0), pair(parity[:, :], 1)
            ad0, ad1 = pair(srt[:, 1, :], 0), pair(srt[:, 1, :], 1)
            nc.vector.tensor_tensor(ctl_row(N_1), new0, new1, ALU.max)
            nc.vector.tensor_tensor(ctl_row(N_2), new0, new1, ALU.mult)
            nc.vector.tensor_scalar(ctl_row(R_2), pair(rank[:, :], 1), -1.0, None, ALU.add)
            nc.vector.tensor_copy(ctl_row(AD_2), ad1)
            nc.vector.tensor_copy(ctl_row(SL_2), par1)
            nc.vector.scalar_tensor_tensor(out=ctl_row(VARIANT), in0=new1, scalar=2.0, in1=par0,
                                           op0=ALU.mult, op1=ALU.add)
            link(nc.vector.tensor_tensor(ctl_row(AD_1), ad0, ad1, ALU.subtract))
            nc.vector.tensor_tensor(ctl_row(R_1), ctl_row(R_2), ctl_row(N_2), ALU.subtract)
            nc.vector.tensor_tensor(ctl_row(SL_1), ctl_row(SL_2), ctl_row(N_2), ALU.not_equal)
            link(nc.vector.tensor_tensor(ctl_row(AD_1), ctl_row(AD_1), ctl_row(N_2), ALU.mult))
            link(nc.vector.tensor_tensor(ctl_row(AD_1), ctl_row(AD_1), ctl_row(AD_2), ALU.add))
            nc.vector.tensor_copy(ctl[:, :, :], ctlf[:, :, :]).then_inc(ctl_ready, 1)
            dve.wait_ge(tok_done, 1)
            link(nc.vector.tensor_copy(tok[:, :, :], psU[:, 0:3 * NT].rearrange("p (n t) -> p n t", n=3)))
            nc.vector.tensor_scalar(notslot[:, :], tok[:, 2, :], -1.0, 1.0, ALU.mult, ALU.add)
            for n in range(NL):
                nc.vector.tensor_scalar(lmask[:, :, n], tok[:, 0, :], float(n), 0.5, ALU.is_equal, ALU.mult)
            link(nc.vector.memset(lbias[:, :], 0.0))

            def prepare(i, src, n, dst, col, loaded, hi_done, before, lo_done):
                weight_scale(i, col, src, n, loaded)
                low_parts(i, src, lambda c, m: dst[:, HI, c:m], lambda c, m: dst[:, LO, c:m], n,
                          wscale[:, col:col + 1], hi_done, before, lo_done)

            def prepare_w3():
                prior = dve.value_load(ctl[0:1, R_2, 0:1], min_val=0, max_val=1) + 1
                prepare(at_w3(prior), raw, WN, w3, W3_, raw_chunks(prior), fixed_hi, SMALL_CHUNKS, fixed_lo)
                link(nc.vector.tensor_scalar(c3[:, :], wscale[:, W3_:W3_ + 1], winv[:, A3_:A3_ + 1], 2.0,
                                             ALU.mult, ALU.mult))

            def prepare_b1():
                dve.wait_ge(b1_loaded, 16 * 3)
                link(nc.vector.tensor_copy(b1[:, :], b1raw))
                low_rows = slice(2 * R1, 3 * R1)
                nc.vector.tensor_tensor(b1[low_rows, :], b1raw[low_rows, :], b1[low_rows, :].bitcast(F32),
                                        ALU.subtract).then_inc(b1_ready, 1)

            def prepare_b3():
                dve.wait_ge(b3_loaded, 16)
                link(nc.vector.tensor_copy(b3[:, HI, :], b3raw))
                nc.vector.tensor_tensor(b3[:, LO, :], b3raw, b3[:, HI, :].bitcast(F32),
                                        ALU.subtract).then_inc(b3_ready, 1)

            prepare(AT_A1, a1raw, K * N1, a1, A1_, [(a_loaded[0], 16)], fixed_hi, 0, fixed_lo)
            prepare(AT_A3, a3raw, K * N3, a3, A3_, [(a_loaded[1], 16)], fixed_hi, 1, fixed_lo)
            prepare(AT_W1, w1raw, WN, w1, W1_, [(semaphore, 16) for semaphore in w1_loaded], whi_ready, 0, wlo_ready)
            link(nc.vector.tensor_tensor(c1[:, :], wscale[:, W1_:W1_ + 1], winv[:, A1_:A1_ + 1], ALU.mult))
            dve.wait_ge(fixed_lo, SMALL_CHUNKS)
            dve.wait_ge(wlo_ready, NCHUNK)

            make_x1(0)
            prepare_b1()
            adapter_event(0, 0, adapter_scale, False)
            make_low(0)
            new_adapters(0, False)
            prepare_b3()
            tile_step(0, True, False)
            with dve.Fori(1, NT - 1) as t:
                tile_step(t, False, False)
            tile_step(NT - 1, False, True)
            make_gates(NT - 1)
            make_out(NT - 1)

        @block.tensor
        def _(pe):
            def layer0(u, tiles_before):
                pe.wait_ge(x_loaded, (u + 1) * 32)
                pe.wait_ge(w0_loaded, (u + 1) * 32)
                if tiles_before == 1:
                    pe.wait_ge(x_ready[0], 1)
                elif tiles_before == 2:
                    pe.wait_ge(x_ready[2], u - 1)
                for n in range(HALVES):
                    cols = slice(n * BANK, n * BANK + BANK)
                    last = nc.tensor.matmul(psZ[:, cols], w0[:, :], xin[:, cols], start=True, stop=True)
                last.then_inc(l0_done, 1)

            def transposes(n, u, free):
                pe.wait_ge(hi_ready[n], u + 1)
                pe.wait_ge(lo_ready[n], u + 1)
                if free is not None:
                    pe.wait_ge(*free)
                for part in (HI, LO):
                    for k in range(K):
                        last = nc.tensor.transpose(psT[:, part, k, :], parts[:, part, k * P:k * P + P], identh[:, :])
                last.then_inc(xT_done[n], 1)

            def projection(xt, w, n, done):
                for k in range(K):
                    for i, (xp, wp) in enumerate(PASSES):
                        last = nc.tensor.matmul(psS[:, 0:n], xt[:, xp, k, :], w[:, wp, k * n:k * n + n],
                                                start=(k == 0 and i == 0), stop=(k == K - 1 and i == 2))
                last.then_inc(done, 1)

            def product(xt, w, n, blocks, chunks_split=False):
                for k in blocks:
                    if chunks_split and k * D % WCHUNK == 0:
                        pe.wait_ge(whi_ready, k * D // WCHUNK + 1)
                        pe.wait_ge(wlo_ready, k * D // WCHUNK + 1)
                    for i, (xp, wp) in enumerate(PASSES):
                        nc.tensor.matmul(psY[:, n * BANK:n * BANK + BANK], xt[:, xp, k, :],
                                         w[:, wp, k * D + n * BANK:k * D + n * BANK + BANK],
                                         start=(k == 0 and i == 0), stop=False)

            BEFORE, AFTER = range(K - 2), range(K - 2, K)

            def low_rank(n, terms, done):
                for i, (lhsT, b) in enumerate(terms):
                    last = nc.tensor.matmul(psY[:, n * BANK:n * BANK + BANK], lhsT, b[:, n * BANK:n * BANK + BANK],
                                            start=False, stop=(i == len(terms) - 1))
                if n == HALVES - 1:
                    last.then_inc(done, 1)

            def layer1(t, tiles_before):
                pe.wait_ge(xT_copied[0], t + 1)
                if tiles_before == 2:
                    pe.wait_ge(hg_ready, t - 1)
                projection(xT[0], a1, N1, la1_done)
                if tiles_before == 2:
                    pe.wait_ge(out_ready, t - 1)
                product(xT[0], w1, 0, range(K), chunks_split=not tiles_before)
                if tiles_before:
                    transposes(2, t - 1, (xT_copied[0], t + 1))
                product(xT[0], w1, 1, BEFORE)
                pe.wait_ge(low_ready, t + 1)
                if tiles_before == 2:
                    pe.wait_ge(hgT_copied, t - 1)
                nc.tensor.transpose(psU[0:3 * R1, 0:P], lowp[:, :, :].rearrange("p a r -> p (a r)").bitcast(F32), ident
                                    ).then_inc(lowT_done, 1)
                product(xT[0], w1, 1, AFTER)
                pe.wait_ge(lowT_copied, t + 1)
                if not tiles_before:
                    pe.wait_ge(b1_ready, 1)
                for n in range(HALVES):
                    low_rank(n, [(lowT[:, :], b1)], l1_done)

            def layer3(v, x1_next, x2_next):
                pe.wait_ge(xT_copied[2], v + 1)
                if x2_next:
                    pe.wait_ge(low_ready, v + 2)
                projection(xT[2], a3, N3, la3_done)
                if x1_next:
                    layer0(v + 2, 2)
                if x2_next:
                    pe.wait_ge(x_ready[1], v + 2)
                product(xT[2], w3, 0, range(K))
                if x2_next:
                    transposes(1, v + 1, (xT_copied[2], v + 1))
                product(xT[2], w3, 1, BEFORE)
                pe.wait_ge(hg_ready, v + 1)
                if x2_next:
                    pe.wait_ge(lowT_copied, v + 2)
                for part in (HI, LO):
                    last = nc.tensor.transpose(psU[:, part * P:part * P + P], hgp[:, part, :].bitcast(F32), ident)
                last.then_inc(hgT_done, 1)
                product(xT[2], w3, 1, AFTER)
                pe.wait_ge(hgT_copied, v + 1)
                for n in range(HALVES):
                    low_rank(n, [(hgT[:, xp, :], b3[:, wp, :]) for xp, wp in PASSES], l3_done)

            def layer2_half(variant, n):
                def weights(slot, part, k):
                    at = (slot * 2 + part) * WN + k * D + n * BANK
                    return w2[:, at:at + BANK]

                for v in range(4):
                    with pe.If(variant == v):
                        for k in range(K):
                            for i, (xp, wp) in enumerate(PASSES):
                                start, stop = k == 0 and i == 0, k == K - 1 and i == 2
                                cols = slice(n * BANK, n * BANK + BANK)
                                if v < 2:
                                    last = nc.tensor.matmul(psZ[:, cols], xT[1][:, xp, k, :], weights(v, wp, k),
                                                            start=start, stop=stop)
                                else:
                                    for h, slot in enumerate((v - 2, 3 - v)):
                                        rows = slice(h * C, h * C + C)
                                        last = nc.tensor.matmul(psZ[rows, cols], xT[1][:, xp, k, rows],
                                                                weights(slot, wp, k), start=start, stop=stop)
                        if n == HALVES - 1:
                            last.then_inc(l2_done, 1)

            def layer2(t, x1_next):
                pe.wait_ge(xT_copied[1], t + 1)
                pe.wait_ge(tile_whi, t + 1)
                pe.wait_ge(tile_wlo, t + 1)
                if x1_next:
                    pe.wait_ge(x_ready[0], t + 2)
                variant = pe.value_load(ctl[0:1, VARIANT, bass.ds(t, 1)], min_val=0, max_val=3)
                layer2_half(variant, 0)
                if x1_next:
                    transposes(0, t + 1, (xT_copied[1], t + 1))
                layer2_half(variant, 1)

            pe.wait_ge(keys_ready, 1)
            for n in range(4):
                last = nc.tensor.matmul(psS[0:1, n * B:n * B + B], vals[:, n:n + 1], perm1h[:, :], start=True, stop=True)
            last.then_inc(sorted_done, 1)
            pe.wait_ge(ctl_ready, 1)
            for n, row in enumerate((srt[:, 2, :], srt[:, 3, :], parity[:, :])):
                for h in range(2):
                    last = nc.tensor.matmul(psU[h * C:h * C + C, n * NT:n * NT + NT], ones[:, 0:C],
                                            row.rearrange("p (t h) -> p h t", h=2)[:, h, :], start=True, stop=True)
            last.then_inc(tok_done, 1)

            layer0(0, 0)
            transposes(0, 0, None)
            pe.wait_ge(fixed_hi, SMALL_CHUNKS)
            pe.wait_ge(fixed_lo, SMALL_CHUNKS)
            layer1(0, 0)
            layer0(1, 1)
            transposes(1, 0, (xT_copied[0], 1))
            layer2(0, True)
            layer1(1, 1)
            pe.wait_ge(fixed_hi, SMALL_CHUNKS + NCHUNK)
            pe.wait_ge(fixed_lo, SMALL_CHUNKS + NCHUNK)
            pe.wait_ge(b3_ready, 1)
            layer3(0, True, True)
            layer2(1, True)
            with pe.Fori(2, NT - 1) as t:
                layer1(t, 2)
                layer3(t - 1, True, True)
                layer2(t, True)
            layer1(NT - 1, 2)
            layer3(NT - 2, False, True)
            layer2(NT - 1, False)
            transposes(2, NT - 1, (xT_copied[1], NT))
            layer3(NT - 1, False, False)


def kernel(**inputs):
    import concourse.bacc as _bacc
    import numpy as _np
    from concourse import mybir as _mybir
    from concourse.bass_utils import run_bass_kernel_spmd as _run

    x = _np.ascontiguousarray(inputs["x"])
    b, c, d = x.shape
    k = d // 128

    def by_contraction(w):
        return _np.ascontiguousarray(w.reshape(w.shape[0], k, 128).transpose(2, 1, 0))

    def flat(w):
        return w.reshape(128, -1)

    nl, _, r1 = inputs["L1_cond_lora_A"].shape
    ne, r3, _ = inputs["L3_cond_A"].shape
    w2 = inputs["L2_cond_weight"]
    na = w2.shape[0]
    a1 = _np.ascontiguousarray(inputs["L1_cond_lora_A"].reshape(nl, k, 128, r1).transpose(2, 1, 0, 3)).reshape(128, k, nl * r1)
    a3 = by_contraction(_np.concatenate([inputs["L3_cond_A"].reshape(ne * r3, d), inputs["L3_cond_Wr"]], 0))
    consts = _np.zeros((128, 128 + b + 1), _np.float32)
    consts[:, 0:128] = _np.eye(128, dtype=_np.float32)
    consts[:, 128:128 + b] = _np.arange(b, dtype=_np.float32)
    consts[:, 128 + b] = _np.arange(128, dtype=_np.float32)
    arrays = {
        "x": x,
        "itok_adapter": _np.ascontiguousarray(inputs["itok_B_0_15"]),
        "itok_label": _np.ascontiguousarray(inputs["itok_B_0_2"]),
        "itok_language": _np.ascontiguousarray(inputs["itok_B_0_7"]),
        "W0": _np.ascontiguousarray(inputs["L0_cond_weights"]),
        "W1": flat(by_contraction(inputs["L1_cond_W"])),
        "A1": a1,
        "B1": _np.ascontiguousarray(inputs["L1_cond_lora_B_w"].T),
        "W2": _np.ascontiguousarray(w2.reshape(na, d, k, 128).transpose(0, 3, 2, 1)).reshape(na, 128, k * d),
        "W3": flat(by_contraction(inputs["L3_cond_W"])),
        "A3": a3,
        "B3": _np.ascontiguousarray(inputs["L3_cond_B"].transpose(0, 2, 1)).reshape(ne * r3, d),
        "consts": consts,
    }
    nc = _bacc.Bacc("TRN2", target_bir_lowering=False, num_devices=1, dynamic_dma_scratch_size=64)
    ap = {n: nc.dram_tensor(f"in_{n}", a.shape, _mybir.dt.from_np(a.dtype), kind="ExternalInput").ap()
          for n, a in arrays.items()}
    out = nc.dram_tensor("out", x.shape, _mybir.dt.float32, kind="ExternalOutput").ap()
    cond_stack_kernel(nc, ap["x"], [ap["itok_adapter"], ap["itok_label"], ap["itok_language"]], ap["W0"], ap["W1"],
                      ap["A1"], ap["B1"], ap["W2"], ap["W3"], ap["A3"], ap["B3"], ap["consts"], out)
    r = _run(nc, [{f"in_{n}": a for n, a in arrays.items()}], core_ids=[0])
    return r.results[0]["out"]
```

```python
from contextlib import ExitStack

import concourse.bass as bass
from concourse import mybir

ALU = mybir.AluOpType
ACT = mybir.ActivationFunctionType
F32 = mybir.dt.float32
F32R = mybir.dt.float32r
F16 = mybir.dt.float16
BF16 = mybir.dt.bfloat16
I32 = mybir.dt.int32
U32 = mybir.dt.uint32
X = mybir.AxisListType.X
ABSMAX = bass.bass_isa.ReduceOp.absmax

P = 128
EXPONENT = 0x7F800000
HI, LO = 0, 1
PASSES = [(HI, HI), (HI, LO), (LO, HI)]
TOP = 14
SCALE_MAX = 2.0 ** 60
WCHUNK = 2048


def cond_stack_kernel(nc, x, ids, W0, W1, A1, B1, W2, W3, A3, B3, shape_consts, out):
    B, C, D = x.shape
    NT = B * C // P
    K = D // P
    R1 = B1.shape[0]
    NL = A1.shape[2] // R1
    N1 = A1.shape[2]
    NE = A3.shape[2] - P
    N3 = A3.shape[2]
    RE = P // NE
    WN = K * D
    BANK = 512
    HALVES = D // BANK
    assert 2 * C == P and NT * 2 == B

    with ExitStack() as ctx:
        def sb(name, shape, dt):
            return ctx.enter_context(nc.sbuf_tensor(name, shape, dt))

        def ps(name, shape, dt):
            return ctx.enter_context(nc.psum_tensor(name, shape, dt))

        def sem(name):
            return ctx.enter_context(nc.semaphore(name))

        w1 = sb("w1", [P, 2, WN], F16)
        w3 = sb("w3", [P, 2, WN], F16)
        w2 = sb("w2", [P, 2 * 2 * WN], F16)
        raw = sb("raw", [P, WN], F32)
        a1 = sb("a1", [P, 2, K * N1], F16)
        a3 = sb("a3", [P, 2, K * N3], F16)
        b1 = sb("b1", [3 * R1, D], F32R)
        b3 = sb("b3", [P, 2, D], F32R)
        w0 = sb("w0", [P, P], F32)
        xs = sb("xs", [P, 4, D], F32)
        xin, x1, x2, x3 = (xs[:, i, :] for i in range(4))
        parts = sb("parts", [P, 2, D], F16)
        xT = [sb(f"x{n}T", [P, 2, K, P], F16) for n in (1, 2, 3)]
        identh = sb("identh", [P, P], F16)
        consts = sb("consts", [P, P + B + 1], F32)
        ident, iotar, iotac = consts[:, 0:P], consts[0:B, P:P + B], consts[0:B, P + B:P + B + 1]
        iotae = consts[:, P:P + NE]
        ones = sb("ones", [1, P], F32)
        rowmax = sb("rowmax", [P, 3], F32)
        expo = sb("expo", [P, 3], F32)
        flip = sb("flip", [P, 3], F32)
        scale = sb("scale", [P, 3], F32)
        unscale = sb("unscale", [P, 3], F32)
        inv3 = sb("inv3", [P, 1], F32)
        NW = 6
        W1_, A1_, W3_, A3_, SLOT = 0, 1, 2, 3, 4
        BOUND = 1024
        partmax = sb("partmax", [P, WN // BOUND], F32)
        wmax = sb("wmax", [P, 2], F32)
        wall = sb("wall", [P, 1], F32)
        onecol = sb("onecol", [P, 1], F32)
        wexpo = sb("wexpo", [P, 1], F32)
        wflip = sb("wflip", [P, 1], F32)
        wscale = sb("wscale", [P, NW], F32)
        winv = sb("winv", [P, NW], F32)
        winvtop = sb("winvtop", [P, NW], F32)
        c1 = sb("c1", [P, 1], F32)
        c3 = sb("c3", [P, 1], F32)
        w2inv = sb("w2inv", [P, 3], F32)
        lowm = sb("lowm", [P, R1, NL], F32)
        low = sb("low", [P, R1], F32)
        lowp = sb("lowp", [P, 3, R1], F32R)
        lowT = sb("lowT", [3 * R1, P], F32R)
        logits = sb("logits", [P, NE], F32)
        top8 = sb("top8", [P, 8], F32)
        topi = sb("topi", [P, 8], U32)
        topf = sb("topf", [P, 8], F32)
        nmax = sb("nmax", [P, 1], F32)
        g = sb("g", [P, 4], F32)
        gates = sb("gates", [P, 2, NE], F32)
        hg = sb("hg", [P, P], F32)
        hgp = sb("hgp", [P, 2, P], F32R)
        hgT = sb("hgT", [P, 2, P], F32R)
        scratch = parts[:, :, :].rearrange("p a n -> p (a n)").bitcast(F32)
        scratch_end = [0]

        def in_parts(rows, cols, dt=F32):
            at, scratch_end[0] = scratch_end[0], scratch_end[0] + cols
            assert scratch_end[0] <= D
            return scratch[0:rows, at:at + cols].bitcast(dt)

        vals = sb("vals", [B, 4], F32)
        keycol = sb("keycol", [B, 1], F32)
        pos = sb("pos", [B, 1], F32)
        keyrow = in_parts(B, B)
        idrow = in_parts(B, B, I32)
        idrowf = in_parts(B, B)
        idcol = sb("idcol", [B, 3], I32)
        before = in_parts(B, B)
        perm1h = in_parts(B, B)
        srt = in_parts(1, 4 * B).rearrange("p (n b) -> p n b", n=4)
        new = in_parts(1, B)
        zrow = in_parts(1, B)
        rank = in_parts(1, B)
        parity = in_parts(1, B)
        VARIANT, N_1, N_2, R_1, R_2, AD_1, AD_2, SL_1, SL_2, NCTL = range(10)
        ctlf = raw[0:1, 0:NCTL * (NT + 1)].rearrange("p (n t) -> p n t", n=NCTL)
        ctl = sb("ctl", [1, NCTL, NT + 1], I32)
        batch = sb("batch", [1, B], I32)
        tok = sb("tok", [P, 3, NT], F32)
        notslot = sb("notslot", [P, NT], F32)
        lmask = sb("lmask", [P, NT, NL], F32)
        lbias = sb("lbias", [P, NE], F32)

        w0id = sb("w0id", [1, B], I32)
        a1raw = xs[:, 1:4, :].rearrange("p a d -> p (a d)")[:, 0:K * N1]
        a3raw = xs[:, 1:4, :].rearrange("p a d -> p (a d)")[:, K * N1:K * (N1 + N3)]
        w1raw = w2[:, 2 * WN:4 * WN].bitcast(F32)
        b1raw = xT[2][0:3 * R1].rearrange("p a k n -> p (a k n)").bitcast(F32)
        b3raw = xT[1][:, :, :, :].rearrange("p a k n -> p (a k n)").bitcast(F32)

        psY = ps("psY", [P, D], F32)
        psZ = ps("psZ", [P, D], F32)
        psT = ps("psT", [P, 2, K, P], F16)
        psS = ps("psS", [P, BANK], F32)
        psU = ps("psU", [P, BANK], F32)

        over_x1T, over_x2T = (xT[n][:, :, :, :].rearrange("p a k n -> p (a k n)").bitcast(BF16) for n in (0, 1))
        over_psT = psT[:, :, :, :].rearrange("p a k n -> p (a k n)").bitcast(F32)

        ids_loaded = sem("ids_loaded")
        b1_loaded, b3_loaded = sem("b1_loaded"), sem("b3_loaded")
        a_loaded = [sem("a1_loaded"), sem("a3_loaded")]
        w1_loaded = [sem(f"w1_loaded{c}") for c in range(WN // WCHUNK)]
        raw_loaded = [sem(f"raw_loaded{c}") for c in range(WN // WCHUNK)]
        x_loaded = sem("x_loaded")
        w0_loaded = sem("w0_loaded")
        stored = sem("stored")
        keys_ready = sem("keys_ready")
        sorted_done = sem("sorted_done")
        ctl_ready = sem("ctl_ready")
        tok_done = sem("tok_done")
        route_chain = sem("route_chain")
        wmax_ready = sem("wmax_ready")
        wall_ready = sem("wall_ready")
        wscale_ready = sem("wscale_ready")
        partmax_ready = sem("partmax_ready")
        fixed_hi, fixed_lo = sem("fixed_hi"), sem("fixed_lo")
        b_chain = sem("b_chain")
        b1_ready, b3_ready = sem("b1_ready"), sem("b3_ready")
        whi_ready = sem("whi_ready")
        wlo_ready = sem("wlo_ready")
        wprep_chain = sem("wprep_chain")
        tile_whi = sem("tile_whi")
        tile_wlo = sem("tile_wlo")
        l0_done, l1_done, l2_done, l3_done = (sem(f"l{n}_done") for n in range(4))
        la1_done, la3_done = sem("la1_done"), sem("la3_done")
        xT_done = [sem(f"x{n}T_done") for n in (1, 2, 3)]
        lowT_done, hgT_done = sem("lowT_done"), sem("hgT_done")
        x_ready = [sem(f"x{n}_ready") for n in (1, 2, 3)]
        scale_ready = [sem(f"scale{n}_ready") for n in (1, 2, 3)]
        lo_ready = [sem(f"lo{n}_ready") for n in (1, 2, 3)]
        hi_ready = [sem(f"hi{n}_ready") for n in (1, 2, 3)]
        xT_copied = [sem(f"x{n}T_copied") for n in (1, 2, 3)]
        low_masked, low_ready, lowT_copied = sem("low_masked"), sem("low_ready"), sem("lowT_copied")
        top_ready, exp_ready, hg_ready, hgT_copied = (
            sem(n) for n in ("top_ready", "exp_ready", "hg_ready", "hgT_copied"))
        out_ready = sem("out_ready")
        scale_chain = [sem(f"scale{n}_chain") for n in (1, 2, 3)]
        gate_chain = sem("gate_chain")
        hg_chain = sem("hg_chain")
        low_chain = sem("low_chain")

        NCHUNK = WN // WCHUNK
        AT_A1, AT_A3, AT_W1 = 0, 1, 2
        UNITS = WN // BOUND

        def at_adapter(prior, later):
            return prior + (4 if later else 3)

        def at_w3(prior):
            return prior + 3

        def split_before(prior):
            return prior * NCHUNK + NCHUNK

        def raw_before(prior, later):
            return prior + 1 if later else prior

        def new_adapter(engine, u, which):
            flag, r, sl = ((N_1, R_1, SL_1), (N_2, R_2, SL_2))[which]
            return (engine.value_load(ctl[0:1, flag, bass.ds(u, 1)], min_val=0, max_val=1),
                    engine.value_load(ctl[0:1, r, bass.ds(u, 1)], min_val=0, max_val=NT),
                    engine.value_load(ctl[0:1, sl, bass.ds(u, 1)], min_val=0, max_val=1))

        def has_second(engine, u):
            return engine.value_load(ctl[0:1, N_2, bass.ds(u, 1)], min_val=0, max_val=1) > 0

        def raw_chunks(before):
            return [(semaphore, before * 16 + 16) for semaphore in raw_loaded]

        SMALL_CHUNKS = 2

        block = ctx.enter_context(nc.Block())

        @block.sync
        def _(sp):
            def load_x(u, batch_of):
                if not (isinstance(u, int) and u == 0):
                    sp.wait_ge(x_ready[0], u)
                for h in range(2):
                    b = batch_of(h)
                    rows = slice(h * C, h * C + C)
                    sp.dma_start(xin[rows, :], x[bass.ds(b, 1)].rearrange("b c d -> (b c) d")
                                 ).then_inc(x_loaded, 16)

            def load_w0(u, adapter_of):
                for h in range(2):
                    rows = slice(h * C, h * C + C)
                    sp.dma_start(w0[rows, rows], W0[bass.ds(adapter_of(h), 1)].rearrange("a c d -> (a c) d")
                                 ).then_inc(w0_loaded, 16)

            def tile_loads(u):
                load_x(u, lambda h: sp.value_load(batch[0:1, bass.ds(2 * u + h, 1)], min_val=0, max_val=B - 1))
                load_w0(u, lambda h: sp.value_load(w0id[0:1, bass.ds(2 * u + h, 1)], min_val=0, max_val=W2.shape[0] - 1))

            def load_adapter(u, which, later=True, after_w3=False):
                flag, r, ad = ((N_1, R_1, AD_1), (N_2, R_2, AD_2))[which]
                n = sp.value_load(ctl[0:1, flag, bass.ds(u, 1)], min_val=0, max_val=1)
                prior = sp.value_load(ctl[0:1, r, bass.ds(u, 1)], min_val=0, max_val=W2.shape[0] - 1)
                a = sp.value_load(ctl[0:1, ad, bass.ds(u, 1)], min_val=0, max_val=W2.shape[0] - 1)
                with sp.If(n > 0):
                    for c in range(NCHUNK):
                        cols = slice(c * WCHUNK, c * WCHUNK + WCHUNK)
                        if after_w3:
                            sp.wait_ge(fixed_hi, SMALL_CHUNKS + c + 1)
                            sp.wait_ge(fixed_lo, SMALL_CHUNKS + c + 1)
                        elif later or which:
                            sp.wait_ge(whi_ready, split_before(prior) - NCHUNK + c + 1)
                            sp.wait_ge(wlo_ready, split_before(prior) - NCHUNK + c + 1)
                        sp.dma_start(raw[:, cols], W2[bass.ds(a, 1)].rearrange("a p n -> (a p) n")[:, cols]
                                     ).then_inc(raw_loaded[c], 16)

            def load_w3():
                prior = sp.value_load(ctl[0:1, R_2, 0:1], min_val=0, max_val=1)
                for c in range(NCHUNK):
                    cols = slice(c * WCHUNK, c * WCHUNK + WCHUNK)
                    sp.wait_ge(whi_ready, split_before(prior) + c + 1)
                    sp.wait_ge(wlo_ready, split_before(prior) + c + 1)
                    sp.dma_start(raw[:, cols], W3[:, cols]).then_inc(raw_loaded[c], 16)

            def store(u):
                sp.wait_ge(out_ready, u + 1)
                for h in range(2):
                    b = sp.value_load(batch[0:1, bass.ds(2 * u + h, 1)], min_val=0, max_val=B - 1)
                    sp.dma_start(out[bass.ds(b, 1)].rearrange("b c d -> (b c) d"), x3[h * C:h * C + C, :]
                                 ).then_inc(stored, 16)

            for n in range(3):
                sp.dma_start(idcol[:, n:n + 1], ids[n].rearrange("(b o) -> b o", o=1)).then_inc(ids_loaded, 16)
            sp.dma_start(idrow[:, :], ids[0].partition_broadcast(B)).then_inc(ids_loaded, 16)
            sp.dma_start(consts[:, :], shape_consts).then_inc(ids_loaded, 16)
            sp.dma_start(a1raw, A1.rearrange("p k n -> p (k n)")).then_inc(a_loaded[0], 16)
            sp.dma_start(a3raw, A3.rearrange("p k n -> p (k n)")).then_inc(a_loaded[1], 16)
            def load_w1(c):
                cols = slice(c * WCHUNK, c * WCHUNK + WCHUNK)
                sp.dma_start(w1raw[:, cols], W1[:, cols]).then_inc(w1_loaded[c], 16)

            load_w1(0)
            sp.wait_ge(ctl_ready, 1)
            tile_loads(0)
            for c in range(1, NCHUNK):
                load_w1(c)
            load_adapter(0, 0, later=False)
            for i in range(3):
                sp.dma_start(b1raw[i * R1:i * R1 + R1, :], B1).then_inc(b1_loaded, 16)
            sp.dma_start(b3raw, B3).then_inc(b3_loaded, 16)
            tile_loads(1)
            load_adapter(0, 1, later=False)
            load_w3()
            load_adapter(1, 0, after_w3=True)
            with sp.Fori(1, NT - 1) as t:
                tile_loads(t + 1)
                load_adapter(t, 1)
                load_adapter(t + 1, 0)
                store(t - 1)
            load_adapter(NT - 1, 1)
            store(NT - 2)
            store(NT - 1)
            sp.wait_ge(stored, 32 * NT)


        @block.gpsimd
        def _(pool):
            def over_partitions(c):
                pool.wait_ge(wmax_ready, c + 1)
                nc.gpsimd.tensor_tensor(wmax[:, 1:2], wmax[:, 0:1], onecol[:, :], ALU.mult)
                pool.drain()
                nc.gpsimd.partition_all_reduce(wall[:, 0:1], wmax[:, 1:2], P, ABSMAX).then_inc(wall_ready, 1)

            nc.gpsimd.memset(onecol[:, :], 1.0)
            pool.drain()
            def new_adapters(u, later):
                n, prior, slot = new_adapter(pool, u, 0)
                with pool.If(n > 0):
                    over_partitions(at_adapter(prior, later))
                with pool.If(has_second(pool, u)):
                    over_partitions(at_adapter(new_adapter(pool, u, 1)[1], later))

            over_partitions(AT_A1)
            over_partitions(AT_A3)
            over_partitions(AT_W1)
            pool.wait_ge(ctl_ready, 1)
            new_adapters(0, False)
            over_partitions(at_w3(pool.value_load(ctl[0:1, R_2, 0:1], min_val=0, max_val=1) + 1))
            with pool.Fori(1, NT) as t:
                new_adapters(t, True)

        @block.scalar
        def _(act):
            def high_parts(chunks, src, dst, n, scale_ap, done):
                for c in chunks:
                    at, m = c * WCHUNK, min(n, c * WCHUNK + WCHUNK)
                    nc.scalar.activation(dst(at, m), src[:, at:m], ACT.Copy, scale=scale_ap).then_inc(done, 1)

            def bound(i, src, n, loaded, over, piece):
                units, per_piece = UNITS * i, piece // BOUND
                for at in range(0, n, piece):
                    if at:
                        act.wait_ge(partmax_ready, units + at // BOUND)
                    elif not (isinstance(i, int) and i == 0):
                        act.wait_ge(wscale_ready, i)
                    if at % WCHUNK == 0:
                        act.wait_ge(*loaded[at // WCHUNK])
                    m = min(n, at + piece)
                    nc.scalar.activation(over[:, 0:m - at], src[:, at:m], ACT.Abs,
                                         accum_out=partmax[:, at // piece:at // piece + 1]
                                         ).then_inc(partmax_ready, per_piece if n > piece else UNITS)
                act.drain()

            def bound_adapter(prior, later, over, piece):
                bound(at_adapter(prior, later), raw, WN, raw_chunks(raw_before(prior, later)), over, piece)

            def high_adapter(prior, slot, later, chunks):
                act.wait_ge(wscale_ready, at_adapter(prior, later) + 1)
                high_parts(chunks, raw, lambda c, m: w2[:, bass.ds(slot * (2 * WN) + c, m - c)], WN,
                           wscale[:, bass.ds(slot + SLOT, 1)], whi_ready)

            def high_part(n, u):
                act.wait_ge(scale_ready[n], u + 1)
                nc.scalar.activation(parts[:, HI, :], (x1, x2, x3)[n], ACT.Copy, scale=scale[:, n:n + 1]
                                     ).then_inc(hi_ready[n], 1)

            def copy_transposed(n, u):
                act.wait_ge(xT_done[n], u + 1)
                nc.scalar.copy(xT[n][:, HI], psT[:, HI])
                nc.scalar.copy(xT[n][:, LO], psT[:, LO]).then_inc(xT_copied[n], 1)

            def copy_lowT(u):
                act.wait_ge(lowT_done, u + 1)
                nc.scalar.copy(lowT[:, :], psU[0:3 * R1, 0:P]).then_inc(lowT_copied, 1)

            def copy_hgT(u):
                act.wait_ge(hgT_done, u + 1)
                nc.scalar.copy(hgT[:, :, :], psU[:, 0:2 * P].rearrange("p (a n) -> p a n", a=2)).then_inc(hgT_copied, 1)

            def gate_exp(u):
                act.wait_ge(top_ready, u + 1)
                nc.scalar.activation(g[:, 0:1], top8[:, 1:2], ACT.Exp, bias=nmax[:, 0:1]).then_inc(exp_ready, 1)

            def tile_step(t, first, last):
                if first:
                    n, prior, slot = new_adapter(act, 0, 0)
                    copy_lowT(0)
                    with act.If(n > 0):
                        high_adapter(prior, slot, False, range(NCHUNK))
                    act.wait_ge(xT_done[0], 1)
                else:
                    n, prior, slot = new_adapter(act, t, 0)
                    copy_transposed(2, t - 1)
                    with act.If(n > 0):
                        high_adapter(prior, slot, True, [3])
                    copy_lowT(t)
                high_part(1, t)
                if not first:
                    gate_exp(t - 1)
                copy_transposed(1, t)
                with act.If(has_second(act, t)):
                    n, prior, slot = new_adapter(act, t, 1)
                    bound_adapter(prior, not first, over_x1T, 2 * BOUND)
                    high_adapter(prior, slot, not first, range(NCHUNK))
                act.drain().then_inc(tile_whi, 1)
                if not first:
                    copy_hgT(t - 1)
                if not last:
                    high_part(0, t + 1)
                if first:
                    third = at_w3(act.value_load(ctl[0:1, R_2, 0:1], min_val=0, max_val=1) + 1)
                    bound(third, raw, WN, raw_chunks(third - 3), over_x1T, 2 * BOUND)
                    copy_transposed(0, 1)
                    high_w3(third, [0, 1])
                    high_part(2, 0)
                    high_w3(third, [2, 3])
                    n, prior, slot = new_adapter(act, 1, 0)
                    with act.If(n > 0):
                        bound_adapter(prior, True, over_x2T, 2 * BOUND)
                        high_adapter(prior, slot, True, [0, 1, 2])
                elif not last:
                    n, prior, slot = new_adapter(act, t + 1, 0)
                    with act.If(n > 0):
                        bound_adapter(prior, True, over_x1T, 2 * BOUND)
                    copy_transposed(0, t + 1)
                    with act.If(n > 0):
                        act.wait_ge(l2_done, t + 1)
                        high_adapter(prior, slot, True, [0])
                    high_part(2, t)
                    with act.If(n > 0):
                        high_adapter(prior, slot, True, [1, 2])
                else:
                    high_part(2, t)

            def high_w3(i, chunks):
                act.wait_ge(wscale_ready, i + 1)
                high_parts(chunks, raw, lambda c, m: w3[:, HI, c:m], WN, wscale[:, W3_:W3_ + 1], fixed_hi)

            bound(AT_A1, a1raw, K * N1, [(a_loaded[0], 16)], over_x1T, 2 * BOUND)
            bound(AT_A3, a3raw, K * N3, [(a_loaded[1], 16)], over_x1T, 2 * BOUND)
            act.wait_ge(wscale_ready, AT_A1 + 1)
            high_parts([0], a1raw, lambda c, m: a1[:, HI, c:m], K * N1, wscale[:, A1_:A1_ + 1], fixed_hi)
            act.wait_ge(wscale_ready, AT_A3 + 1)
            high_parts([0], a3raw, lambda c, m: a3[:, HI, c:m], K * N3, wscale[:, A3_:A3_ + 1], fixed_hi)
            bound(AT_W1, w1raw, WN, [(semaphore, 16) for semaphore in w1_loaded], over_x1T, 2 * BOUND)
            high_part(0, 0)
            act.wait_ge(wscale_ready, AT_W1 + 1)
            high_parts([0, 1], w1raw, lambda c, m: w1[:, HI, c:m], WN, wscale[:, W1_:W1_ + 1], whi_ready)
            copy_transposed(0, 0)
            high_parts([2, 3], w1raw, lambda c, m: w1[:, HI, c:m], WN, wscale[:, W1_:W1_ + 1], whi_ready)
            act.wait_ge(ctl_ready, 1)
            act.wait_ge(xT_copied[0], 1)
            n, prior, _ = new_adapter(act, 0, 0)
            with act.If(n > 0):
                bound_adapter(prior, False, over_psT, BOUND)
            tile_step(0, True, False)
            with act.Fori(1, NT - 1) as t:
                tile_step(t, False, False)
            tile_step(NT - 1, False, True)
            copy_transposed(2, NT - 1)
            gate_exp(NT - 1)
            copy_hgT(NT - 1)

        @block.vector
        def _(dve):
            def scale_from(maxima, e, f, chain, base):
                nc.vector.tensor_scalar(f.bitcast(I32), maxima.bitcast(I32), EXPONENT, EXPONENT,
                                        ALU.bitwise_and, ALU.bitwise_xor).then_inc(chain, 1)
                nc.vector.tensor_scalar(e.bitcast(I32), maxima.bitcast(I32), EXPONENT, None,
                                        ALU.bitwise_and).then_inc(chain, 1)
                dve.wait_ge(chain, base + 2)

            WLINKS = 4

            def weight_scale(i, col, pieces):
                dve.wait_ge(partmax_ready, i * UNITS + UNITS)
                nc.vector.tensor_reduce(wmax[:, 0:1], partmax[:, 0:pieces], X, ALU.max).then_inc(wmax_ready, 1)
                dve.wait_ge(wall_ready, i + 1)
                base = i * WLINKS
                scale_from(wall[:, 0:1], wexpo[:, :], wflip[:, :], wprep_chain, base)
                at = bass.ds(col, 1)
                nc.vector.tensor_scalar(winv[:, at], wexpo[:, :], 2.0 ** TOP / SCALE_MAX, 2.0 ** -TOP,
                                        ALU.max, ALU.mult).then_inc(wprep_chain, 1)
                nc.vector.tensor_scalar(winvtop[:, at], wexpo[:, :], 2.0 ** TOP / SCALE_MAX, 2.0 ** (-2 * TOP),
                                        ALU.max, ALU.mult).then_inc(wprep_chain, 1)
                nc.vector.tensor_scalar(wscale[:, at], wflip[:, :], 2.0 ** (TOP - 1), SCALE_MAX,
                                        ALU.mult, ALU.min).then_inc(wscale_ready, 1)

            def low_parts(i, src, hi, lo, n, scale_ap, hi_done, hi_base, lo_done, chunks):
                dve.wait_ge(wprep_chain, i * WLINKS + WLINKS)
                dve.wait_ge(wscale_ready, i + 1)
                for j in chunks:
                    c, m = j * WCHUNK, min(n, j * WCHUNK + WCHUNK)
                    dve.wait_ge(hi_done, hi_base + j + 1)
                    nc.vector.scalar_tensor_tensor(out=lo(c, m), in0=src[:, c:m], scalar=scale_ap, in1=hi(c, m),
                                                   op0=ALU.mult, op1=ALU.subtract).then_inc(lo_done, 1)

            def adapter_scale(prior, slot, later, pieces=WN // (2 * BOUND)):
                weight_scale(at_adapter(prior, later), slot + SLOT, pieces)

            def adapter_low(prior, slot, later, chunks):
                low_parts(at_adapter(prior, later), raw, lambda c, m: w2[:, bass.ds(slot * (2 * WN) + c, m - c)],
                          lambda c, m: w2[:, bass.ds(slot * (2 * WN) + (WN + c), m - c)], WN,
                          wscale[:, bass.ds(slot + SLOT, 1)], whi_ready, split_before(prior), wlo_ready, chunks)

            def second_adapter(u, later):
                with dve.If(has_second(dve, u)):
                    n, prior, slot = new_adapter(dve, u, 1)
                    adapter_scale(prior, slot, later)
                    adapter_low(prior, slot, later, range(NCHUNK))
                dve.drain().then_inc(tile_wlo, 1)

            ROWLINKS = (4, 6, 5)

            def split_rows(n, u):
                split_scale(n, u)
                split_low(n, u)

            def split_scale(n, u):
                src = (x1, x2, x3)[n]
                base = u * ROWLINKS[n]
                dve.wait_ge(x_ready[n], u + 1)
                nc.vector.tensor_reduce(rowmax[:, n:n + 1], src, X, ALU.max, apply_absolute_value=True
                                        ).then_inc(scale_chain[n], 1)
                dve.wait_ge(scale_chain[n], base + 1)
                e, f = expo[:, n:n + 1], flip[:, n:n + 1]
                scale_from(rowmax[:, n:n + 1], e, f, scale_chain[n], base + 1)
                nc.vector.tensor_scalar(scale[:, n:n + 1], f, 2.0 ** (TOP - 1), SCALE_MAX,
                                        ALU.mult, ALU.min).then_inc(scale_ready[n], 1)
                if n == 1:
                    nc.vector.tensor_tensor(w2inv[:, 0:1], winvtop[:, SLOT:SLOT + 1], notslot[:, bass.ds(u, 1)],
                                            ALU.mult).then_inc(scale_chain[n], 1)
                    dve.wait_ge(scale_chain[n], base + 4)
                    nc.vector.scalar_tensor_tensor(out=w2inv[:, 1:2], in0=winvtop[:, SLOT + 1:SLOT + 2],
                                                   scalar=tok[:, 2, bass.ds(u, 1)], in1=w2inv[:, 0:1],
                                                   op0=ALU.mult, op1=ALU.add).then_inc(scale_chain[n], 1)
                    dve.wait_ge(scale_chain[n], base + 5)

            def split_low(n, u):
                src = (x1, x2, x3)[n]
                base = u * ROWLINKS[n]
                e = expo[:, n:n + 1]
                by = (winvtop[:, W1_:W1_ + 1], w2inv[:, 1:2], winvtop[:, W3_:W3_ + 1])[n]
                nc.vector.tensor_scalar(unscale[:, n:n + 1], e, 2.0 ** TOP / SCALE_MAX, by,
                                        ALU.max, ALU.mult).then_inc(scale_chain[n], 1)
                if n == 2:
                    nc.vector.tensor_scalar(inv3[:, :], e, 2.0 ** TOP / SCALE_MAX, winvtop[:, A3_:A3_ + 1],
                                            ALU.max, ALU.mult).then_inc(scale_chain[n], 1)
                dve.wait_ge(hi_ready[n], u + 1)
                dve.wait_ge(scale_ready[n], u + 1)
                dve.wait_ge(scale_chain[n], base + ROWLINKS[n])
                nc.vector.scalar_tensor_tensor(out=parts[:, LO, :], in0=src, scalar=scale[:, n:n + 1],
                                               in1=parts[:, HI, :], op0=ALU.mult, op1=ALU.subtract
                                               ).then_inc(lo_ready[n], 1)

            def make_x1(u):
                dve.wait_ge(l0_done, u + 1)
                nc.vector.tensor_tensor(x1, psZ[:, :], xin, ALU.add).then_inc(x_ready[0], 1)
                split_rows(0, u)

            def make_x2(u):
                dve.wait_ge(l1_done, u + 1)
                nc.vector.scalar_tensor_tensor(out=x2, in0=psY[:, :], scalar=unscale[:, 0:1], in1=x1,
                                               op0=ALU.mult, op1=ALU.add).then_inc(x_ready[1], 1)
                split_rows(1, u)

            def make_x3(u, first):
                dve.wait_ge(l2_done, u + 1)
                if not first:
                    dve.wait_ge(stored, u * 32)
                nc.vector.scalar_tensor_tensor(out=x3, in0=psZ[:, :], scalar=unscale[:, 1:2], in1=x2,
                                               op0=ALU.mult, op1=ALU.add).then_inc(x_ready[2], 1)
                split_rows(2, u)

            def make_out(u):
                dve.wait_ge(l3_done, u + 1)
                nc.vector.scalar_tensor_tensor(out=x3, in0=psY[:, :], scalar=unscale[:, 2:3], in1=x3,
                                               op0=ALU.mult, op1=ALU.add).then_inc(out_ready, 1)

            def make_low(u):
                dve.wait_ge(la1_done, u + 1)
                nc.vector.scalar_tensor_tensor(
                    out=lowm[:, :, :], in0=psS[:, 0:N1].rearrange("p (l r) -> p r l", l=NL), scalar=c1[:, 0:1],
                    in1=lmask[:, bass.ds(u, 1), :].to_broadcast([P, R1, NL]),
                    op0=ALU.mult, op1=ALU.mult).then_inc(low_masked, 1)
                dve.wait_ge(low_masked, u + 1)
                nc.vector.tensor_reduce(low[:, :], lowm[:, :, :], X, ALU.add).then_inc(low_chain, 1)
                dve.wait_ge(low_chain, u * 2 + 1)
                nc.vector.tensor_copy(lowp[:, 2, :], low[:, :])
                nc.vector.tensor_copy(lowp[:, 0, :], low[:, :]).then_inc(low_chain, 1)
                dve.wait_ge(low_chain, u * 2 + 2)
                nc.vector.tensor_tensor(lowp[:, 1, :], low[:, :], lowp[:, 0, :].bitcast(F32), ALU.subtract
                                        ).then_inc(low_ready, 1)

            GLINKS = 11

            def make_gates(u):
                base = u * GLINKS
                nc.vector.tensor_scalar(lbias[:, :], iotae, tok[:, 1, bass.ds(u, 1)], 5.0, ALU.is_equal, ALU.mult
                                        ).then_inc(gate_chain, 1)
                dve.wait_ge(gate_chain, base + 1)
                dve.wait_ge(la3_done, u + 1)
                nc.vector.scalar_tensor_tensor(out=logits[:, :], in0=psS[:, P:N3], scalar=inv3[:, 0:1],
                                               in1=lbias[:, :],
                                               op0=ALU.mult, op1=ALU.add).then_inc(gate_chain, 1)
                dve.drain()
                nc.vector.max(top8[:, :], logits[:, :]).then_inc(gate_chain, 1)
                dve.wait_ge(gate_chain, base + 3)
                nc.vector.tensor_scalar(nmax[:, :], top8[:, 0:1], -1.0, None, ALU.mult).then_inc(top_ready, 1)
                nc.vector.max_index(topi[:, :], top8[:, :], logits[:, :]).then_inc(gate_chain, 1)
                dve.wait_ge(gate_chain, base + 4)
                nc.vector.tensor_copy(topf[:, :], topi[:, :]).then_inc(gate_chain, 1)
                dve.wait_ge(exp_ready, u + 1)
                nc.vector.tensor_scalar(g[:, 1:2], g[:, 0:1], 1.0, None, ALU.add).then_inc(gate_chain, 1)
                dve.wait_ge(gate_chain, base + 6)
                nc.vector.reciprocal(g[:, 2:3], g[:, 1:2]).then_inc(gate_chain, 1)
                dve.wait_ge(gate_chain, base + 7)
                nc.vector.tensor_scalar(g[:, 3:4], g[:, 2:3], g[:, 0:1], c3[:, 0:1], ALU.mult, ALU.mult
                                        ).then_inc(gate_chain, 1)
                nc.vector.tensor_scalar(gates[:, 0, :], iotae, topf[:, 0:1], g[:, 2:3], ALU.is_equal, ALU.mult
                                        ).then_inc(gate_chain, 1)
                dve.wait_ge(gate_chain, base + 9)
                nc.vector.tensor_scalar(gates[:, 1, :], iotae, topf[:, 1:2], g[:, 3:4], ALU.is_equal, ALU.mult
                                        ).then_inc(gate_chain, 1)
                dve.wait_ge(gate_chain, base + 10)
                nc.vector.scalar_tensor_tensor(out=gates[:, 0, :], in0=gates[:, 0, :], scalar=c3[:, 0:1],
                                               in1=gates[:, 1, :], op0=ALU.mult, op1=ALU.add
                                               ).then_inc(gate_chain, 1)
                dve.wait_ge(gate_chain, base + 11)
                nc.vector.tensor_tensor(hg[:, :].rearrange("p (e r) -> p e r", e=NE),
                                        psS[:, 0:P].rearrange("p (e r) -> p e r", e=NE),
                                        gates[:, 0, :].unsqueeze(2).to_broadcast([P, NE, RE]),
                                        ALU.mult).then_inc(hg_chain, 1)
                dve.wait_ge(hg_chain, u * 2 + 1)
                nc.vector.tensor_copy(hgp[:, HI, :], hg[:, :]).then_inc(hg_chain, 1)
                dve.wait_ge(hg_chain, u * 2 + 2)
                nc.vector.tensor_tensor(hgp[:, LO, :], hg[:, :], hgp[:, HI, :].bitcast(F32), ALU.subtract
                                        ).then_inc(hg_ready, 1)

            def tile_step(t, first, last):
                n, prior, slot = new_adapter(dve, t, 0)
                make_x2(t)
                if not first:
                    make_gates(t - 1)
                with dve.If(n > 0):
                    adapter_low(prior, slot, not first, [NCHUNK - 1])
                second_adapter(t, not first)
                if not last:
                    make_x1(t + 1)
                if first:
                    prepare_w3()
                    n, prior, slot = new_adapter(dve, 1, 0)
                    make_low(1)
                    with dve.If(n > 0):
                        adapter_scale(prior, slot, True)
                        adapter_low(prior, slot, True, range(NCHUNK - 1))
                elif last:
                    make_out(t - 1)
                    make_x3(t, False)
                else:
                    n, prior, slot = new_adapter(dve, t + 1, 0)
                    make_out(t - 1)
                    with dve.If(n > 0):
                        adapter_scale(prior, slot, True)
                    make_x3(t, False)
                    make_low(t + 1)
                    with dve.If(n > 0):
                        adapter_low(prior, slot, True, range(NCHUNK - 1))

            links = [0]

            def link(ins):
                ins.then_inc(route_chain, 1)
                links[0] += 1
                dve.wait_ge(route_chain, links[0])

            nc.vector.memset(ones[:, :], 1.0)
            nc.vector.memset(winvtop[:, :], 1.0)
            nc.vector.memset(zrow[:, :], 0.0)
            nc.vector.memset(new[:, 0:1], 1.0)
            nc.vector.memset(ctlf[:, :, :], 0.0)
            link(nc.vector.memset(w0[:, :], 0.0))
            dve.wait_ge(ids_loaded, 16 * 5)
            nc.vector.tensor_copy(identh[:, :], ident)
            nc.vector.tensor_copy(vals[:, 0:1], iotac)
            nc.vector.tensor_copy(vals[:, 1:4], idcol[:, :])
            link(nc.vector.tensor_copy(idrowf[:, :], idrow[:, :]))
            nc.vector.scalar_tensor_tensor(out=keyrow[:, :], in0=idrowf[:, :], scalar=float(B), in1=iotar,
                                           op0=ALU.mult, op1=ALU.add)
            link(nc.vector.scalar_tensor_tensor(out=keycol[:, :], in0=vals[:, 1:2], scalar=float(B), in1=iotac,
                                                op0=ALU.mult, op1=ALU.add))
            link(nc.vector.tensor_scalar(before[:, :], keyrow[:, :], keycol[:, 0:1], None, ALU.is_lt))
            link(nc.vector.tensor_reduce(pos[:, :], before[:, :], X, ALU.add))
            nc.vector.tensor_scalar(perm1h[:, :], iotar, pos[:, 0:1], None, ALU.is_equal).then_inc(keys_ready, 1)
            dve.wait_ge(sorted_done, 1)
            link(nc.vector.tensor_copy(srt[:, :, :], psS[0:1, 0:4 * B].rearrange("p (n b) -> p n b", n=4)))
            nc.vector.tensor_copy(batch[:, :], srt[:, 0, :])
            nc.vector.tensor_copy(w0id[:, :], srt[:, 1, :])
            link(nc.vector.tensor_tensor(new[:, 1:B], srt[:, 1, 1:B], srt[:, 1, 0:B - 1], ALU.not_equal))
            nc.vector.tensor_tensor_scan(rank[:, :], new[:, :], zrow[:, :], 0.0, ALU.add, ALU.add)
            nc.vector.tensor_tensor_scan(parity[:, :], new[:, :], zrow[:, :], 1.0, ALU.not_equal, ALU.add
                                         ).then_inc(route_chain, 1)
            links[0] += 1
            dve.wait_ge(route_chain, links[0])

            def pair(row, h):
                return row.rearrange("p (t h) -> p h t", h=2)[:, h, :]

            def ctl_row(n):
                return ctlf[:, n, 0:NT]

            new0, new1 = pair(new[:, :], 0), pair(new[:, :], 1)
            par0, par1 = pair(parity[:, :], 0), pair(parity[:, :], 1)
            ad0, ad1 = pair(srt[:, 1, :], 0), pair(srt[:, 1, :], 1)
            nc.vector.tensor_tensor(ctl_row(N_1), new0, new1, ALU.max)
            nc.vector.tensor_tensor(ctl_row(N_2), new0, new1, ALU.mult)
            nc.vector.tensor_scalar(ctl_row(R_2), pair(rank[:, :], 1), -1.0, None, ALU.add)
            nc.vector.tensor_copy(ctl_row(AD_2), ad1)
            nc.vector.tensor_copy(ctl_row(SL_2), par1)
            nc.vector.scalar_tensor_tensor(out=ctl_row(VARIANT), in0=new1, scalar=2.0, in1=par0,
                                           op0=ALU.mult, op1=ALU.add)
            link(nc.vector.tensor_tensor(ctl_row(AD_1), ad0, ad1, ALU.subtract))
            nc.vector.tensor_tensor(ctl_row(R_1), ctl_row(R_2), ctl_row(N_2), ALU.subtract)
            nc.vector.tensor_tensor(ctl_row(SL_1), ctl_row(SL_2), ctl_row(N_2), ALU.not_equal)
            link(nc.vector.tensor_tensor(ctl_row(AD_1), ctl_row(AD_1), ctl_row(N_2), ALU.mult))
            link(nc.vector.tensor_tensor(ctl_row(AD_1), ctl_row(AD_1), ctl_row(AD_2), ALU.add))
            nc.vector.tensor_copy(ctl[:, :, :], ctlf[:, :, :]).then_inc(ctl_ready, 1)
            dve.wait_ge(tok_done, 1)
            link(nc.vector.tensor_copy(tok[:, :, :], psU[:, 0:3 * NT].rearrange("p (n t) -> p n t", n=3)))
            nc.vector.tensor_scalar(notslot[:, :], tok[:, 2, :], -1.0, 1.0, ALU.mult, ALU.add)
            for n in range(NL):
                nc.vector.tensor_scalar(lmask[:, :, n], tok[:, 0, :], float(n), 0.5, ALU.is_equal, ALU.mult)
            link(nc.vector.memset(lbias[:, :], 0.0))

            def fixed_low(i, src, n, dst, col, hi_done, before, lo_done):
                low_parts(i, src, lambda c, m: dst[:, HI, c:m], lambda c, m: dst[:, LO, c:m], n,
                          wscale[:, col:col + 1], hi_done, before, lo_done, range(-(-n // WCHUNK)))

            def low_w3(prior, chunks):
                low_parts(at_w3(prior), raw, lambda c, m: w3[:, HI, c:m], lambda c, m: w3[:, LO, c:m], WN,
                          wscale[:, W3_:W3_ + 1], fixed_hi, SMALL_CHUNKS, fixed_lo, chunks)

            def prepare_w3():
                prior = dve.value_load(ctl[0:1, R_2, 0:1], min_val=0, max_val=1) + 1
                weight_scale(at_w3(prior), W3_, WN // (2 * BOUND))
                low_w3(prior, [0, 1])
                make_x3(0, True)
                low_w3(prior, [2, 3])
                link(nc.vector.tensor_scalar(c3[:, :], wscale[:, W3_:W3_ + 1], winv[:, A3_:A3_ + 1], 2.0,
                                             ALU.mult, ALU.mult))

            def prepare_b1():
                dve.wait_ge(b1_loaded, 16 * 3)
                link(nc.vector.tensor_copy(b1[:, :], b1raw))
                low_rows = slice(2 * R1, 3 * R1)
                nc.vector.tensor_tensor(b1[low_rows, :], b1raw[low_rows, :], b1[low_rows, :].bitcast(F32),
                                        ALU.subtract).then_inc(b1_ready, 1)

            def prepare_b3():
                dve.wait_ge(b3_loaded, 16)
                link(nc.vector.tensor_copy(b3[:, HI, :], b3raw))
                nc.vector.tensor_tensor(b3[:, LO, :], b3raw, b3[:, HI, :].bitcast(F32),
                                        ALU.subtract).then_inc(b3_ready, 1)

            weight_scale(AT_A1, A1_, 1)
            fixed_low(AT_A1, a1raw, K * N1, a1, A1_, fixed_hi, 0, fixed_lo)
            weight_scale(AT_A3, A3_, 1)
            fixed_low(AT_A3, a3raw, K * N3, a3, A3_, fixed_hi, 1, fixed_lo)
            dve.wait_ge(fixed_lo, SMALL_CHUNKS)
            dve.wait_ge(l0_done, 1)
            nc.vector.tensor_tensor(x1, psZ[:, :], xin, ALU.add).then_inc(x_ready[0], 1)
            split_scale(0, 0)
            weight_scale(AT_W1, W1_, WN // (2 * BOUND))
            dve.wait_ge(wprep_chain, AT_W1 * WLINKS + WLINKS)
            split_low(0, 0)
            fixed_low(AT_W1, w1raw, WN, w1, W1_, whi_ready, 0, wlo_ready)
            link(nc.vector.tensor_tensor(c1[:, :], wscale[:, W1_:W1_ + 1], winv[:, A1_:A1_ + 1], ALU.mult))
            dve.wait_ge(wlo_ready, NCHUNK)

            prepare_b1()
            make_low(0)
            n, prior, slot = new_adapter(dve, 0, 0)
            with dve.If(n > 0):
                adapter_scale(prior, slot, False, WN // BOUND)
                adapter_low(prior, slot, False, range(NCHUNK - 1))
            prepare_b3()
            tile_step(0, True, False)
            with dve.Fori(1, NT - 1) as t:
                tile_step(t, False, False)
            tile_step(NT - 1, False, True)
            make_gates(NT - 1)
            make_out(NT - 1)

        @block.tensor
        def _(pe):
            def layer0(u, tiles_before):
                pe.wait_ge(x_loaded, (u + 1) * 32)
                pe.wait_ge(w0_loaded, (u + 1) * 32)
                if tiles_before == 1:
                    pe.wait_ge(x_ready[0], 1)
                elif tiles_before == 2:
                    pe.wait_ge(x_ready[2], u - 1)
                for n in range(HALVES):
                    cols = slice(n * BANK, n * BANK + BANK)
                    last = nc.tensor.matmul(psZ[:, cols], w0[:, :], xin[:, cols], start=True, stop=True)
                last.then_inc(l0_done, 1)

            def transposes(n, u, free):
                pe.wait_ge(hi_ready[n], u + 1)
                pe.wait_ge(lo_ready[n], u + 1)
                if free is not None:
                    pe.wait_ge(*free)
                for part in (HI, LO):
                    for k in range(K):
                        last = nc.tensor.transpose(psT[:, part, k, :], parts[:, part, k * P:k * P + P], identh[:, :])
                last.then_inc(xT_done[n], 1)

            def projection(xt, w, n, done):
                for k in range(K):
                    for i, (xp, wp) in enumerate(PASSES):
                        last = nc.tensor.matmul(psS[:, 0:n], xt[:, xp, k, :], w[:, wp, k * n:k * n + n],
                                                start=(k == 0 and i == 0), stop=(k == K - 1 and i == 2))
                last.then_inc(done, 1)

            def product(xt, w, n, blocks, chunks_split=False):
                for k in blocks:
                    if chunks_split and k * D % WCHUNK == 0:
                        pe.wait_ge(whi_ready, k * D // WCHUNK + 1)
                        pe.wait_ge(wlo_ready, k * D // WCHUNK + 1)
                    for i, (xp, wp) in enumerate(PASSES):
                        nc.tensor.matmul(psY[:, n * BANK:n * BANK + BANK], xt[:, xp, k, :],
                                         w[:, wp, k * D + n * BANK:k * D + n * BANK + BANK],
                                         start=(k == 0 and i == 0), stop=False)

            BEFORE, AFTER = range(K - 2), range(K - 2, K)

            def low_rank(n, terms, done):
                for i, (lhsT, b) in enumerate(terms):
                    last = nc.tensor.matmul(psY[:, n * BANK:n * BANK + BANK], lhsT, b[:, n * BANK:n * BANK + BANK],
                                            start=False, stop=(i == len(terms) - 1))
                if n == HALVES - 1:
                    last.then_inc(done, 1)

            def layer1(t, tiles_before):
                pe.wait_ge(xT_copied[0], t + 1)
                if tiles_before == 2:
                    pe.wait_ge(hg_ready, t - 1)
                projection(xT[0], a1, N1, la1_done)
                if tiles_before == 2:
                    pe.wait_ge(out_ready, t - 1)
                product(xT[0], w1, 0, range(K), chunks_split=not tiles_before)
                if tiles_before:
                    transposes(2, t - 1, (xT_copied[0], t + 1))
                product(xT[0], w1, 1, BEFORE)
                pe.wait_ge(low_ready, t + 1)
                if tiles_before == 2:
                    pe.wait_ge(hgT_copied, t - 1)
                nc.tensor.transpose(psU[0:3 * R1, 0:P], lowp[:, :, :].rearrange("p a r -> p (a r)").bitcast(F32), ident
                                    ).then_inc(lowT_done, 1)
                product(xT[0], w1, 1, AFTER)
                pe.wait_ge(lowT_copied, t + 1)
                if not tiles_before:
                    pe.wait_ge(b1_ready, 1)
                for n in range(HALVES):
                    low_rank(n, [(lowT[:, :], b1)], l1_done)

            def layer3(v, x1_next, x2_next):
                pe.wait_ge(xT_copied[2], v + 1)
                if x2_next:
                    pe.wait_ge(low_ready, v + 2)
                projection(xT[2], a3, N3, la3_done)
                if x1_next:
                    layer0(v + 2, 2)
                if x2_next:
                    pe.wait_ge(x_ready[1], v + 2)
                product(xT[2], w3, 0, range(K))
                if x2_next:
                    transposes(1, v + 1, (xT_copied[2], v + 1))
                product(xT[2], w3, 1, BEFORE)
                pe.wait_ge(hg_ready, v + 1)
                if x2_next:
                    pe.wait_ge(lowT_copied, v + 2)
                for part in (HI, LO):
                    last = nc.tensor.transpose(psU[:, part * P:part * P + P], hgp[:, part, :].bitcast(F32), ident)
                last.then_inc(hgT_done, 1)
                product(xT[2], w3, 1, AFTER)
                pe.wait_ge(hgT_copied, v + 1)
                for n in range(HALVES):
                    low_rank(n, [(hgT[:, xp, :], b3[:, wp, :]) for xp, wp in PASSES], l3_done)

            def layer2_half(variant, n):
                def weights(slot, part, k):
                    at = (slot * 2 + part) * WN + k * D + n * BANK
                    return w2[:, at:at + BANK]

                for v in range(4):
                    with pe.If(variant == v):
                        for k in range(K):
                            for i, (xp, wp) in enumerate(PASSES):
                                start, stop = k == 0 and i == 0, k == K - 1 and i == 2
                                cols = slice(n * BANK, n * BANK + BANK)
                                if v < 2:
                                    last = nc.tensor.matmul(psZ[:, cols], xT[1][:, xp, k, :], weights(v, wp, k),
                                                            start=start, stop=stop)
                                else:
                                    for h, slot in enumerate((v - 2, 3 - v)):
                                        rows = slice(h * C, h * C + C)
                                        last = nc.tensor.matmul(psZ[rows, cols], xT[1][:, xp, k, rows],
                                                                weights(slot, wp, k), start=start, stop=stop)
                        if n == HALVES - 1:
                            last.then_inc(l2_done, 1)

            def layer2(t, x1_next):
                pe.wait_ge(xT_copied[1], t + 1)
                pe.wait_ge(tile_whi, t + 1)
                pe.wait_ge(tile_wlo, t + 1)
                if x1_next:
                    pe.wait_ge(x_ready[0], t + 2)
                variant = pe.value_load(ctl[0:1, VARIANT, bass.ds(t, 1)], min_val=0, max_val=3)
                layer2_half(variant, 0)
                if x1_next:
                    transposes(0, t + 1, (xT_copied[1], t + 1))
                layer2_half(variant, 1)

            pe.wait_ge(keys_ready, 1)
            for n in range(4):
                last = nc.tensor.matmul(psS[0:1, n * B:n * B + B], vals[:, n:n + 1], perm1h[:, :], start=True, stop=True)
            last.then_inc(sorted_done, 1)
            pe.wait_ge(ctl_ready, 1)
            for n, row in enumerate((srt[:, 2, :], srt[:, 3, :], parity[:, :])):
                for h in range(2):
                    last = nc.tensor.matmul(psU[h * C:h * C + C, n * NT:n * NT + NT], ones[:, 0:C],
                                            row.rearrange("p (t h) -> p h t", h=2)[:, h, :], start=True, stop=True)
            last.then_inc(tok_done, 1)

            layer0(0, 0)
            transposes(0, 0, None)
            pe.wait_ge(fixed_hi, SMALL_CHUNKS)
            pe.wait_ge(fixed_lo, SMALL_CHUNKS)
            layer1(0, 0)
            layer0(1, 1)
            transposes(1, 0, (xT_copied[0], 1))
            layer2(0, True)
            layer1(1, 1)
            pe.wait_ge(fixed_hi, SMALL_CHUNKS + NCHUNK)
            pe.wait_ge(fixed_lo, SMALL_CHUNKS + NCHUNK)
            pe.wait_ge(b3_ready, 1)
            layer3(0, True, True)
            layer2(1, True)
            with pe.Fori(2, NT - 1) as t:
                layer1(t, 2)
                layer3(t - 1, True, True)
                layer2(t, True)
            layer1(NT - 1, 2)
            layer3(NT - 2, False, True)
            layer2(NT - 1, False)
            transposes(2, NT - 1, (xT_copied[1], NT))
            layer3(NT - 1, False, False)


def kernel(**inputs):
    import concourse.bacc as _bacc
    import numpy as _np
    from concourse import mybir as _mybir
    from concourse.bass_utils import run_bass_kernel_spmd as _run

    x = _np.ascontiguousarray(inputs["x"])
    b, c, d = x.shape
    k = d // 128

    def by_contraction(w):
        return _np.ascontiguousarray(w.reshape(w.shape[0], k, 128).transpose(2, 1, 0))

    def flat(w):
        return w.reshape(128, -1)

    nl, _, r1 = inputs["L1_cond_lora_A"].shape
    ne, r3, _ = inputs["L3_cond_A"].shape
    w2 = inputs["L2_cond_weight"]
    na = w2.shape[0]
    a1 = _np.ascontiguousarray(inputs["L1_cond_lora_A"].reshape(nl, k, 128, r1).transpose(2, 1, 0, 3)).reshape(128, k, nl * r1)
    a3 = by_contraction(_np.concatenate([inputs["L3_cond_A"].reshape(ne * r3, d), inputs["L3_cond_Wr"]], 0))
    consts = _np.zeros((128, 128 + b + 1), _np.float32)
    consts[:, 0:128] = _np.eye(128, dtype=_np.float32)
    consts[:, 128:128 + b] = _np.arange(b, dtype=_np.float32)
    consts[:, 128 + b] = _np.arange(128, dtype=_np.float32)
    arrays = {
        "x": x,
        "itok_adapter": _np.ascontiguousarray(inputs["itok_B_0_15"]),
        "itok_label": _np.ascontiguousarray(inputs["itok_B_0_2"]),
        "itok_language": _np.ascontiguousarray(inputs["itok_B_0_7"]),
        "W0": _np.ascontiguousarray(inputs["L0_cond_weights"]),
        "W1": flat(by_contraction(inputs["L1_cond_W"])),
        "A1": a1,
        "B1": _np.ascontiguousarray(inputs["L1_cond_lora_B_w"].T),
        "W2": _np.ascontiguousarray(w2.reshape(na, d, k, 128).transpose(0, 3, 2, 1)).reshape(na, 128, k * d),
        "W3": flat(by_contraction(inputs["L3_cond_W"])),
        "A3": a3,
        "B3": _np.ascontiguousarray(inputs["L3_cond_B"].transpose(0, 2, 1)).reshape(ne * r3, d),
        "consts": consts,
    }
    nc = _bacc.Bacc("TRN2", target_bir_lowering=False, num_devices=1, dynamic_dma_scratch_size=64)
    ap = {n: nc.dram_tensor(f"in_{n}", a.shape, _mybir.dt.from_np(a.dtype), kind="ExternalInput").ap()
          for n, a in arrays.items()}
    out = nc.dram_tensor("out", x.shape, _mybir.dt.float32, kind="ExternalOutput").ap()
    cond_stack_kernel(nc, ap["x"], [ap["itok_adapter"], ap["itok_label"], ap["itok_language"]], ap["W0"], ap["W1"],
                      ap["A1"], ap["B1"], ap["W2"], ap["W3"], ap["A3"], ap["B3"], ap["consts"], out)
    r = _run(nc, [{f"in_{n}": a for n, a in arrays.items()}], core_ids=[0])
    return r.results[0]["out"]
```

```python
from contextlib import ExitStack

import concourse.bass as bass
from concourse import mybir

ALU = mybir.AluOpType
ACT = mybir.ActivationFunctionType
F32 = mybir.dt.float32
F32R = mybir.dt.float32r
F16 = mybir.dt.float16
BF16 = mybir.dt.bfloat16
I32 = mybir.dt.int32
U32 = mybir.dt.uint32
X = mybir.AxisListType.X
ABSMAX = bass.bass_isa.ReduceOp.absmax

P = 128
EXPONENT = 0x7F800000
HI, LO = 0, 1
PASSES = [(HI, HI), (HI, LO), (LO, HI)]
TOP = 14
SCALE_MAX = 2.0 ** 60
WCHUNK = 2048


def cond_stack_kernel(nc, x, ids, W0, W1, A1, B1, W2, W3, A3, B3, shape_consts, out):
    B, C, D = x.shape
    NT = B * C // P
    K = D // P
    R1 = B1.shape[0]
    NL = A1.shape[2] // R1
    N1 = A1.shape[2]
    NE = A3.shape[2] - P
    N3 = A3.shape[2]
    RE = P // NE
    WN = K * D
    BANK = 512
    HALVES = D // BANK
    assert 2 * C == P and NT * 2 == B

    with ExitStack() as ctx:
        def sb(name, shape, dt):
            return ctx.enter_context(nc.sbuf_tensor(name, shape, dt))

        def ps(name, shape, dt):
            return ctx.enter_context(nc.psum_tensor(name, shape, dt))

        def sem(name):
            return ctx.enter_context(nc.semaphore(name))

        w1 = sb("w1", [P, 2, WN], F16)
        w3 = sb("w3", [P, 2, WN], F16)
        w2 = sb("w2", [P, 2 * 2 * WN], F16)
        raw = sb("raw", [P, WN], F32)
        a1 = sb("a1", [P, 2, K * N1], F16)
        a3 = sb("a3", [P, 2, K * N3], F16)
        b1 = sb("b1", [3 * R1, D], F32R)
        b3 = sb("b3", [P, 2, D], F32R)
        w0 = sb("w0", [P, P], F32)
        xs = sb("xs", [P, 4, D], F32)
        xin, x1, x2, x3 = (xs[:, i, :] for i in range(4))
        parts = sb("parts", [P, 2, D], F16)
        xT = [sb(f"x{n}T", [P, 2, K, P], F16) for n in (1, 2, 3)]
        identh = sb("identh", [P, P], F16)
        consts = sb("consts", [P, P + B + 1], F32)
        ident, iotar, iotac = consts[:, 0:P], consts[0:B, P:P + B], consts[0:B, P + B:P + B + 1]
        iotae = consts[:, P:P + NE]
        ones = sb("ones", [1, P], F32)
        rowmax = sb("rowmax", [P, 3], F32)
        expo = sb("expo", [P, 3], F32)
        flip = sb("flip", [P, 3], F32)
        scale = sb("scale", [P, 3], F32)
        unscale = sb("unscale", [P, 4], F32)
        inv3 = sb("inv3", [P, 1], F32)
        NW = 6
        W1_, A1_, W3_, A3_, SLOT = 0, 1, 2, 3, 4
        FROM_A1, FROM_A3, FROM_W1, FROM_E = 4, 5, 6, 10
        partmax = sb("partmax", [P, 14], F32)
        wmax = sb("wmax", [P, 2], F32)
        wall = sb("wall", [P, 1], F32)
        onecol = sb("onecol", [P, 1], F32)
        wexpo = sb("wexpo", [P, 1], F32)
        wflip = sb("wflip", [P, 1], F32)
        wscale = sb("wscale", [P, NW], F32)
        winv = sb("winv", [P, NW], F32)
        winvtop = sb("winvtop", [P, NW], F32)
        c1 = sb("c1", [P, 1], F32)
        c3 = sb("c3", [P, 1], F32)
        w2inv = sb("w2inv", [P, 3], F32)
        lowm = sb("lowm", [P, R1, NL], F32)
        low = sb("low", [P, R1], F32)
        lowp = sb("lowp", [P, 3, R1], F32R)
        lowT = sb("lowT", [3 * R1, P], F32R)
        logits = sb("logits", [P, NE], F32)
        top8 = sb("top8", [P, 8], F32)
        topi = sb("topi", [P, 8], U32)
        topf = sb("topf", [P, 8], F32)
        nmax = sb("nmax", [P, 1], F32)
        g = sb("g", [P, 4], F32)
        gates = sb("gates", [P, 2, NE], F32)
        hg = sb("hg", [P, P], F32)
        hgp = sb("hgp", [P, 2, P], F32R)
        hgT = sb("hgT", [P, 2, P], F32R)
        scratch = parts[:, :, :].rearrange("p a n -> p (a n)").bitcast(F32)
        scratch_end = [0]

        def in_parts(rows, cols, dt=F32):
            at, scratch_end[0] = scratch_end[0], scratch_end[0] + cols
            assert scratch_end[0] <= D
            return scratch[0:rows, at:at + cols].bitcast(dt)

        vals = sb("vals", [B, 4], F32)
        keycol = sb("keycol", [B, 1], F32)
        pos = sb("pos", [B, 1], F32)
        keyrow = in_parts(B, B)
        idrow = in_parts(B, B, I32)
        idrowf = in_parts(B, B)
        idcol = sb("idcol", [B, 3], I32)
        before = in_parts(B, B)
        perm1h = in_parts(B, B)
        srt = in_parts(1, 4 * B).rearrange("p (n b) -> p n b", n=4)
        new = in_parts(1, B)
        zrow = in_parts(1, B)
        rank = in_parts(1, B)
        parity = in_parts(1, B)
        VARIANT, N_1, N_2, R_1, R_2, AD_1, AD_2, SL_1, SL_2, NCTL = range(10)
        ctlf = raw[0:1, 0:NCTL * (NT + 1)].rearrange("p (n t) -> p n t", n=NCTL)
        ctl = sb("ctl", [1, NCTL, NT + 1], I32)
        batch = sb("batch", [1, B], I32)
        tok = sb("tok", [P, 3, NT], F32)
        notslot = sb("notslot", [P, NT], F32)
        lmask = sb("lmask", [P, NT, NL], F32)
        lbias = sb("lbias", [P, NE], F32)

        w0id = sb("w0id", [1, B], I32)
        a1raw = xs[:, 1:4, :].rearrange("p a d -> p (a d)")[:, 0:K * N1]
        a3raw = xs[:, 1:4, :].rearrange("p a d -> p (a d)")[:, K * N1:K * (N1 + N3)]
        w1raw = w2[:, 2 * WN:4 * WN].bitcast(F32)
        b1raw = xT[1][0:3 * R1].rearrange("p a k n -> p (a k n)").bitcast(F32)
        b3raw = xT[2][:, :, :, :].rearrange("p a k n -> p (a k n)").bitcast(F32)

        psY = ps("psY", [P, D], F32)
        psZ = ps("psZ", [P, D], F32)
        psT = ps("psT", [P, 2, K, P], F16)
        psS = ps("psS", [P, BANK], F32)
        psU = ps("psU", [P, BANK], F32)

        over_x1T, over_x2T = (xT[n][:, :, :, :].rearrange("p a k n -> p (a k n)").bitcast(BF16) for n in (0, 1))

        def over_w3(place):
            return w3[:, :, :].rearrange("p a n -> p (a n)")[:, place * WCHUNK:place * WCHUNK + WCHUNK].bitcast(BF16)

        ids_loaded = sem("ids_loaded")
        b1_loaded, b3_loaded = sem("b1_loaded"), sem("b3_loaded")
        a_loaded = [sem("a1_loaded"), sem("a3_loaded")]
        w1_loaded = [sem(f"w1_loaded{c}") for c in range(WN // WCHUNK)]
        raw_loaded = [sem(f"raw_loaded{c}") for c in range(WN // WCHUNK)]
        x_loaded = sem("x_loaded")
        w0_loaded = sem("w0_loaded")
        stored = sem("stored")
        keys_ready = sem("keys_ready")
        sorted_done = sem("sorted_done")
        ctl_ready = sem("ctl_ready")
        tok_done = sem("tok_done")
        route_chain = sem("route_chain")
        wmax_ready = sem("wmax_ready")
        wall_ready = sem("wall_ready")
        wscale_ready = sem("wscale_ready")
        partmax_ready = sem("partmax_ready")
        chunkmax_ready = sem("chunkmax_ready")
        fixed_hi, fixed_lo = sem("fixed_hi"), sem("fixed_lo")
        b_chain = sem("b_chain")
        b1_ready, b3_ready = sem("b1_ready"), sem("b3_ready")
        whi_ready = sem("whi_ready")
        wlo_ready = sem("wlo_ready")
        wprep_chain = sem("wprep_chain")
        tile_whi = sem("tile_whi")
        tile_wlo = sem("tile_wlo")
        l0_done, l1_done, l2_done, l3_done = (sem(f"l{n}_done") for n in range(4))
        la1_done, la3_done = sem("la1_done"), sem("la3_done")
        xT_done = [sem(f"x{n}T_done") for n in (1, 2, 3)]
        lowT_done, hgT_done = sem("lowT_done"), sem("hgT_done")
        x_ready = [sem(f"x{n}_ready") for n in (1, 2, 3)]
        scale_ready = [sem(f"scale{n}_ready") for n in (1, 2, 3)]
        lo_ready = [sem(f"lo{n}_ready") for n in (1, 2, 3)]
        hi_ready = [sem(f"hi{n}_ready") for n in (1, 2, 3)]
        xT_copied = [sem(f"x{n}T_copied") for n in (1, 2, 3)]
        low_masked, low_ready, lowT_copied = sem("low_masked"), sem("low_ready"), sem("lowT_copied")
        top_ready, exp_ready, hg_ready, hgT_copied = (
            sem(n) for n in ("top_ready", "exp_ready", "hg_ready", "hgT_copied"))
        out_ready = sem("out_ready")
        scale_chain = [sem(f"scale{n}_chain") for n in (1, 2, 3)]
        unscale_chain = sem("unscale_chain")
        unscale_ready = [sem(f"unscale{n}_ready") for n in (1, 2, 3)]
        inv3_ready = sem("inv3_ready")
        gate_chain = sem("gate_chain")
        hg_chain = sem("hg_chain")
        low_chain = sem("low_chain")

        NCHUNK = WN // WCHUNK
        AT_A1, AT_A3, AT_W1 = 0, 1, 2
        UNITS = NCHUNK
        AT_E = 3

        def at_adapter(prior, later):
            return prior + (4 if later else 3)

        def at_w3(prior):
            return prior + 3

        def split_before(prior):
            return prior * NCHUNK + NCHUNK

        def raw_before(prior, later):
            return prior + 1 if later else prior

        def new_adapter(engine, u, which):
            flag, r, sl = ((N_1, R_1, SL_1), (N_2, R_2, SL_2))[which]
            return (engine.value_load(ctl[0:1, flag, bass.ds(u, 1)], min_val=0, max_val=1),
                    engine.value_load(ctl[0:1, r, bass.ds(u, 1)], min_val=0, max_val=NT),
                    engine.value_load(ctl[0:1, sl, bass.ds(u, 1)], min_val=0, max_val=1))

        def has_second(engine, u):
            return engine.value_load(ctl[0:1, N_2, bass.ds(u, 1)], min_val=0, max_val=1) > 0

        def is_last(u):
            return isinstance(u, int) and u == NT - 1

        def x3_of(u):
            return xin if is_last(u) else x3

        def unscale_of(n, u):
            column = 3 if n == 2 and is_last(u) else n
            return unscale[:, column:column + 1]

        def raw_chunks(before):
            return [(semaphore, before * 16 + 16) for semaphore in raw_loaded]

        SMALL_CHUNKS = 2

        block = ctx.enter_context(nc.Block())

        @block.sync
        def _(sp):
            def load_x(u, batch_of):
                if not (isinstance(u, int) and u == 0):
                    sp.wait_ge(x_ready[0], u)
                for h in range(2):
                    b = batch_of(h)
                    rows = slice(h * C, h * C + C)
                    sp.dma_start(xin[rows, :], x[bass.ds(b, 1)].rearrange("b c d -> (b c) d")
                                 ).then_inc(x_loaded, 16)

            def load_w0(u, adapter_of):
                for h in range(2):
                    rows = slice(h * C, h * C + C)
                    sp.dma_start(w0[rows, rows], W0[bass.ds(adapter_of(h), 1)].rearrange("a c d -> (a c) d")
                                 ).then_inc(w0_loaded, 16)

            def tile_loads(u):
                load_x(u, lambda h: sp.value_load(batch[0:1, bass.ds(2 * u + h, 1)], min_val=0, max_val=B - 1))
                load_w0(u, lambda h: sp.value_load(w0id[0:1, bass.ds(2 * u + h, 1)], min_val=0, max_val=W2.shape[0] - 1))

            def load_adapter(u, which, later=True, after_w3=False):
                flag, r, ad = ((N_1, R_1, AD_1), (N_2, R_2, AD_2))[which]
                n = sp.value_load(ctl[0:1, flag, bass.ds(u, 1)], min_val=0, max_val=1)
                prior = sp.value_load(ctl[0:1, r, bass.ds(u, 1)], min_val=0, max_val=W2.shape[0] - 1)
                a = sp.value_load(ctl[0:1, ad, bass.ds(u, 1)], min_val=0, max_val=W2.shape[0] - 1)
                with sp.If(n > 0):
                    for c in range(NCHUNK):
                        cols = slice(c * WCHUNK, c * WCHUNK + WCHUNK)
                        if after_w3:
                            sp.wait_ge(fixed_hi, SMALL_CHUNKS + c + 1)
                            sp.wait_ge(fixed_lo, SMALL_CHUNKS + c + 1)
                        elif later or which:
                            sp.wait_ge(whi_ready, split_before(prior) - NCHUNK + c + 1)
                            sp.wait_ge(wlo_ready, split_before(prior) - NCHUNK + c + 1)
                        sp.dma_start(raw[:, cols], W2[bass.ds(a, 1)].rearrange("a p n -> (a p) n")[:, cols]
                                     ).then_inc(raw_loaded[c], 16)

            def load_w3():
                prior = sp.value_load(ctl[0:1, R_2, 0:1], min_val=0, max_val=1)
                for c in range(NCHUNK):
                    cols = slice(c * WCHUNK, c * WCHUNK + WCHUNK)
                    sp.wait_ge(whi_ready, split_before(prior) + c + 1)
                    sp.wait_ge(wlo_ready, split_before(prior) + c + 1)
                    sp.dma_start(raw[:, cols], W3[:, cols]).then_inc(raw_loaded[c], 16)

            def store(u):
                sp.wait_ge(out_ready, u + 1)
                for h in range(2):
                    b = sp.value_load(batch[0:1, bass.ds(2 * u + h, 1)], min_val=0, max_val=B - 1)
                    sp.dma_start(out[bass.ds(b, 1)].rearrange("b c d -> (b c) d"), x3_of(u)[h * C:h * C + C, :]
                                 ).then_inc(stored, 16)

            for n in range(3):
                sp.dma_start(idcol[:, n:n + 1], ids[n].rearrange("(b o) -> b o", o=1)).then_inc(ids_loaded, 16)
            sp.dma_start(idrow[:, :], ids[0].partition_broadcast(B)).then_inc(ids_loaded, 16)
            sp.dma_start(consts[:, :], shape_consts).then_inc(ids_loaded, 16)
            sp.dma_start(a1raw, A1.rearrange("p k n -> p (k n)")).then_inc(a_loaded[0], 16)
            sp.dma_start(a3raw, A3.rearrange("p k n -> p (k n)")).then_inc(a_loaded[1], 16)
            def load_w1(c):
                cols = slice(c * WCHUNK, c * WCHUNK + WCHUNK)
                sp.dma_start(w1raw[:, cols], W1[:, cols]).then_inc(w1_loaded[c], 16)

            load_w1(0)
            load_w1(1)
            sp.wait_ge(ctl_ready, 1)
            tile_loads(0)
            load_w1(2)
            load_w1(3)
            for i in range(3):
                sp.dma_start(b1raw[i * R1:i * R1 + R1, :], B1).then_inc(b1_loaded, 16)
            load_adapter(0, 0, later=False)
            sp.dma_start(b3raw, B3).then_inc(b3_loaded, 16)
            tile_loads(1)
            load_adapter(0, 1, later=False)
            tile_loads(2)
            load_w3()
            load_adapter(1, 0, after_w3=True)
            load_adapter(1, 1)
            load_adapter(2, 0)
            store(0)
            with sp.Fori(2, NT - 1) as t:
                tile_loads(t + 1)
                load_adapter(t, 1)
                load_adapter(t + 1, 0)
                store(t - 1)
            load_adapter(NT - 1, 1)
            store(NT - 2)
            store(NT - 1)
            sp.wait_ge(stored, 32 * NT)


        @block.gpsimd
        def _(pool):
            def over_partitions(c):
                pool.wait_ge(wmax_ready, c + 1)
                nc.gpsimd.tensor_tensor(wmax[:, 1:2], wmax[:, 0:1], onecol[:, :], ALU.mult)
                pool.drain()
                nc.gpsimd.partition_all_reduce(wall[:, 0:1], wmax[:, 1:2], P, ABSMAX).then_inc(wall_ready, 1)

            nc.gpsimd.memset(onecol[:, :], 1.0)
            pool.drain()
            def second_adapter(u, later):
                with pool.If(has_second(pool, u)):
                    over_partitions(at_adapter(new_adapter(pool, u, 1)[1], later))

            over_partitions(AT_A1)
            over_partitions(AT_A3)
            over_partitions(AT_W1)
            over_partitions(AT_E)
            pool.wait_ge(ctl_ready, 1)
            second_adapter(0, False)
            over_partitions(at_w3(pool.value_load(ctl[0:1, R_2, 0:1], min_val=0, max_val=1) + 1))
            with pool.Fori(1, NT) as t:
                n, prior, _ = new_adapter(pool, t, 0)
                with pool.If(n > 0):
                    over_partitions(at_adapter(prior, True))
                second_adapter(t, True)

        @block.scalar
        def _(act):
            def high_parts(chunks, src, dst, n, scale_ap, done):
                for c in chunks:
                    at, m = c * WCHUNK, min(n, c * WCHUNK + WCHUNK)
                    nc.scalar.activation(dst(at, m), src[:, at:m], ACT.Copy, scale=scale_ap).then_inc(done, 1)

            def bound_chunk(c, src, n, loaded, over, column, adds=1):
                at, m = c * WCHUNK, min(n, c * WCHUNK + WCHUNK)
                act.wait_ge(*loaded)
                nc.scalar.activation(over[:, 0:m - at], src[:, at:m], ACT.Abs, accum_out=partmax[:, column:column + 1]
                                     ).then_inc(partmax_ready, adds)

            def bound_adapter(prior, later, over, chunks=range(NCHUNK)):
                i = at_adapter(prior, later)
                for c in chunks:
                    if c == 0:
                        act.wait_ge(wscale_ready, i)
                    else:
                        act.wait_ge(partmax_ready, i * UNITS + c)
                    bound_chunk(c, raw, WN, raw_chunks(raw_before(prior, later))[c], over, c)
                act.drain()

            def high_adapter(prior, slot, later, chunks):
                act.wait_ge(wscale_ready, at_adapter(prior, later) + 1)
                high_parts(chunks, raw, lambda c, m: w2[:, bass.ds(slot * (2 * WN) + c, m - c)], WN,
                           wscale[:, bass.ds(slot + SLOT, 1)], whi_ready)

            def high_part(n, u):
                act.wait_ge(scale_ready[n], u + 1)
                nc.scalar.activation(parts[:, HI, :], (x1, x2, x3_of(u))[n], ACT.Copy, scale=scale[:, n:n + 1]
                                     ).then_inc(hi_ready[n], 1)

            def copy_transposed(n, u):
                act.wait_ge(xT_done[n], u + 1)
                nc.scalar.copy(xT[n][:, HI], psT[:, HI])
                nc.scalar.copy(xT[n][:, LO], psT[:, LO]).then_inc(xT_copied[n], 1)

            def copy_lowT(u):
                act.wait_ge(lowT_done, u + 1)
                nc.scalar.copy(lowT[:, :], psU[0:3 * R1, 0:P]).then_inc(lowT_copied, 1)

            def copy_hgT(u):
                act.wait_ge(hgT_done, u + 1)
                nc.scalar.copy(hgT[:, :, :], psU[:, 0:2 * P].rearrange("p (a n) -> p a n", a=2)).then_inc(hgT_copied, 1)

            def gate_exp(u):
                act.wait_ge(top_ready, u + 1)
                nc.scalar.activation(g[:, 0:1], top8[:, 1:2], ACT.Exp, bias=nmax[:, 0:1]).then_inc(exp_ready, 1)

            def second_adapter(u, later):
                with act.If(has_second(act, u)):
                    n, prior, slot = new_adapter(act, u, 1)
                    bound_adapter(prior, later, over_x1T)
                    high_adapter(prior, slot, later, range(NCHUNK))
                act.drain().then_inc(tile_whi, 1)

            def high_w1(chunks):
                act.wait_ge(wscale_ready, AT_W1 + 1)
                high_parts(chunks, w1raw, lambda c, m: w1[:, HI, c:m], WN, wscale[:, W1_:W1_ + 1], whi_ready)

            def high_w3(i, chunks):
                act.wait_ge(wscale_ready, i + 1)
                high_parts(chunks, raw, lambda c, m: w3[:, HI, c:m], WN, wscale[:, W3_:W3_ + 1], fixed_hi)

            def high_small(i, raw_i, dst, n, column):
                act.wait_ge(wscale_ready, i + 1)
                high_parts([0], raw_i, lambda c, m: dst[:, HI, c:m], n, wscale[:, column:column + 1], fixed_hi)

            def bound_w1(c):
                bound_chunk(c, w1raw, WN, (w1_loaded[c], 16), over_w3(c), FROM_W1 + c, 1 + c // 2)

            bound_chunk(0, a1raw, K * N1, (a_loaded[0], 16), over_w3(4), FROM_A1, UNITS)
            bound_chunk(0, a3raw, K * N3, (a_loaded[1], 16), over_w3(5), FROM_A3, UNITS)
            bound_w1(0)
            high_small(AT_A1, a1raw, a1, K * N1, A1_)
            high_small(AT_A3, a3raw, a3, K * N3, A3_)
            bound_w1(1)
            bound_w1(2)
            high_part(0, 0)
            high_w1([0])
            copy_transposed(0, 0)
            high_w1([1, 2, 3])

            for c in range(NCHUNK - 1):
                bound_chunk(c, raw, WN, raw_chunks(0)[c], over_w3(5 + c), FROM_E + c, 1 + c // 2)
            copy_lowT(0)
            high_adapter(0, 0, False, [0])
            act.wait_ge(xT_done[0], 1)
            high_part(1, 0)
            high_adapter(0, 0, False, [1])
            copy_transposed(1, 0)
            high_part(0, 1)
            high_adapter(0, 0, False, [2, 3])
            act.wait_ge(ctl_ready, 1)
            second_adapter(0, False)

            third = at_w3(act.value_load(ctl[0:1, R_2, 0:1], min_val=0, max_val=1) + 1)
            act.wait_ge(wscale_ready, third)
            for c in range(NCHUNK):
                if c == NCHUNK // 2:
                    copy_transposed(0, 1)
                bound_chunk(c, raw, WN, raw_chunks(third - 3)[c], over_w3(4 + c), c)
            high_part(2, 0)
            high_w3(third, [0, 1])
            copy_transposed(2, 0)
            high_w3(third, [2])
            copy_lowT(1)
            high_w3(third, [3])

            n, prior, slot = new_adapter(act, 1, 0)
            with act.If(n > 0):
                bound_adapter(prior, True, over_x2T, [0, 1])
            high_part(1, 1)
            with act.If(n > 0):
                bound_adapter(prior, True, over_x2T, [2, 3])
            gate_exp(0)
            copy_transposed(1, 1)
            with act.If(n > 0):
                high_adapter(prior, slot, True, [0])
            high_part(0, 2)
            copy_hgT(0)
            with act.If(n > 0):
                high_adapter(prior, slot, True, [1, 2, 3])
            second_adapter(1, True)

            def tile_end(t):
                n, prior, slot = new_adapter(act, t + 1, 0)
                with act.If(n > 0):
                    bound_adapter(prior, True, over_x1T)
                copy_transposed(0, t + 1)
                with act.If(n > 0):
                    act.wait_ge(l2_done, t + 1)
                    high_adapter(prior, slot, True, [0])
                high_part(2, t)
                with act.If(n > 0):
                    high_adapter(prior, slot, True, [1, 2])

            tile_end(1)

            def tile_step(t, last):
                n, prior, slot = new_adapter(act, t, 0)
                copy_transposed(2, t - 1)
                with act.If(n > 0):
                    high_adapter(prior, slot, True, [3])
                copy_lowT(t)
                high_part(1, t)
                gate_exp(t - 1)
                copy_transposed(1, t)
                second_adapter(t, True)
                copy_hgT(t - 1)
                if last:
                    high_part(2, t)
                    return
                high_part(0, t + 1)
                tile_end(t)

            with act.Fori(2, NT - 1) as t:
                tile_step(t, False)
            tile_step(NT - 1, True)
            copy_transposed(2, NT - 1)
            gate_exp(NT - 1)
            copy_hgT(NT - 1)

        @block.vector
        def _(dve):
            def scale_from(maxima, e, f, chain, base):
                nc.vector.tensor_scalar(f.bitcast(I32), maxima.bitcast(I32), EXPONENT, EXPONENT,
                                        ALU.bitwise_and, ALU.bitwise_xor).then_inc(chain, 1)
                nc.vector.tensor_scalar(e.bitcast(I32), maxima.bitcast(I32), EXPONENT, None,
                                        ALU.bitwise_and).then_inc(chain, 1)
                dve.wait_ge(chain, base + 2)

            WLINKS = 4

            def weight_scale(i, col, column=0, pieces=NCHUNK):
                weight_max(i, column, pieces)
                weight_scale_end(i, col)

            def weight_max(i, column, pieces=NCHUNK):
                dve.wait_ge(partmax_ready, i * UNITS + UNITS)
                nc.vector.tensor_reduce(wmax[:, 0:1], partmax[:, column:column + pieces], X, ALU.max).then_inc(wmax_ready, 1)

            def weight_scale_end(i, col):
                dve.wait_ge(wall_ready, i + 1)
                base = i * WLINKS
                scale_from(wall[:, 0:1], wexpo[:, :], wflip[:, :], wprep_chain, base)
                at = bass.ds(col, 1)
                nc.vector.tensor_scalar(winv[:, at], wexpo[:, :], 2.0 ** TOP / SCALE_MAX, 2.0 ** -TOP,
                                        ALU.max, ALU.mult).then_inc(wprep_chain, 1)
                nc.vector.tensor_scalar(winvtop[:, at], wexpo[:, :], 2.0 ** TOP / SCALE_MAX, 2.0 ** (-2 * TOP),
                                        ALU.max, ALU.mult).then_inc(wprep_chain, 1)
                nc.vector.tensor_scalar(wscale[:, at], wflip[:, :], 2.0 ** (TOP - 1), SCALE_MAX,
                                        ALU.mult, ALU.min).then_inc(wscale_ready, 1)

            def low_parts(i, src, hi, lo, n, scale_ap, hi_done, hi_base, lo_done, chunks):
                dve.wait_ge(wprep_chain, i * WLINKS + WLINKS)
                dve.wait_ge(wscale_ready, i + 1)
                for j in chunks:
                    c, m = j * WCHUNK, min(n, j * WCHUNK + WCHUNK)
                    dve.wait_ge(hi_done, hi_base + j + 1)
                    nc.vector.scalar_tensor_tensor(out=lo(c, m), in0=src[:, c:m], scalar=scale_ap, in1=hi(c, m),
                                                   op0=ALU.mult, op1=ALU.subtract).then_inc(lo_done, 1)

            def adapter_scale(prior, slot, later):
                weight_scale(at_adapter(prior, later), slot + SLOT)

            def adapter_low(prior, slot, later, chunks):
                low_parts(at_adapter(prior, later), raw, lambda c, m: w2[:, bass.ds(slot * (2 * WN) + c, m - c)],
                          lambda c, m: w2[:, bass.ds(slot * (2 * WN) + (WN + c), m - c)], WN,
                          wscale[:, bass.ds(slot + SLOT, 1)], whi_ready, split_before(prior), wlo_ready, chunks)

            def second_adapter(u, later):
                with dve.If(has_second(dve, u)):
                    n, prior, slot = new_adapter(dve, u, 1)
                    adapter_scale(prior, slot, later)
                    adapter_low(prior, slot, later, range(NCHUNK))
                dve.drain().then_inc(tile_wlo, 1)

            ROWLINKS, UNSCALELINKS = 3, 2

            def split_rows(n, u):
                split_scale(n, u)
                split_low(n, u)

            def rows_of(n, u):
                return (x1, x2, x3_of(u))[n]

            def split_scale(n, u):
                src = rows_of(n, u)
                base = u * ROWLINKS
                dve.wait_ge(x_ready[n], u + 1)
                nc.vector.tensor_reduce(rowmax[:, n:n + 1], src, X, ALU.max, apply_absolute_value=True
                                        ).then_inc(scale_chain[n], 1)
                dve.wait_ge(scale_chain[n], base + 1)
                e, f = expo[:, n:n + 1], flip[:, n:n + 1]
                scale_from(rowmax[:, n:n + 1], e, f, scale_chain[n], base + 1)
                nc.vector.tensor_scalar(scale[:, n:n + 1], f, 2.0 ** (TOP - 1), SCALE_MAX,
                                        ALU.mult, ALU.min).then_inc(scale_ready[n], 1)

            def row_unscale(n, u):
                base = u * UNSCALELINKS
                if n == 1:
                    nc.vector.tensor_tensor(w2inv[:, 0:1], winvtop[:, SLOT:SLOT + 1], notslot[:, bass.ds(u, 1)],
                                            ALU.mult).then_inc(unscale_chain, 1)
                    dve.wait_ge(unscale_chain, base + 1)
                    nc.vector.scalar_tensor_tensor(out=w2inv[:, 1:2], in0=winvtop[:, SLOT + 1:SLOT + 2],
                                                   scalar=tok[:, 2, bass.ds(u, 1)], in1=w2inv[:, 0:1],
                                                   op0=ALU.mult, op1=ALU.add).then_inc(unscale_chain, 1)
                    dve.wait_ge(unscale_chain, base + 2)
                by = (winvtop[:, W1_:W1_ + 1], w2inv[:, 1:2], winvtop[:, W3_:W3_ + 1])[n]
                nc.vector.tensor_scalar(unscale_of(n, u), expo[:, n:n + 1], 2.0 ** TOP / SCALE_MAX, by,
                                        ALU.max, ALU.mult).then_inc(unscale_ready[n], 1)

            def split_low(n, u):
                src = rows_of(n, u)
                if n != 1 and not (isinstance(u, int) and u == 0):
                    row_unscale(n, u)
                if n == 2:
                    nc.vector.tensor_scalar(inv3[:, :], expo[:, n:n + 1], 2.0 ** TOP / SCALE_MAX,
                                            winvtop[:, A3_:A3_ + 1], ALU.max, ALU.mult).then_inc(inv3_ready, 1)
                dve.wait_ge(hi_ready[n], u + 1)
                dve.wait_ge(scale_ready[n], u + 1)
                nc.vector.scalar_tensor_tensor(out=parts[:, LO, :], in0=src, scalar=scale[:, n:n + 1],
                                               in1=parts[:, HI, :], op0=ALU.mult, op1=ALU.subtract
                                               ).then_inc(lo_ready[n], 1)

            def make_x1(u):
                dve.wait_ge(l0_done, u + 1)
                nc.vector.tensor_tensor(x1, psZ[:, :], xin, ALU.add).then_inc(x_ready[0], 1)
                split_rows(0, u)

            def make_x2(u):
                dve.wait_ge(l1_done, u + 1)
                dve.wait_ge(unscale_ready[0], u + 1)
                nc.vector.scalar_tensor_tensor(out=x2, in0=psY[:, :], scalar=unscale[:, 0:1], in1=x1,
                                               op0=ALU.mult, op1=ALU.add).then_inc(x_ready[1], 1)
                split_rows(1, u)

            def make_x3(u, first):
                add_x3(u, first)
                split_rows(2, u)

            def add_x3(u, first):
                dve.wait_ge(l2_done, u + 1)
                dve.wait_ge(unscale_ready[1], u + 1)
                if not (first or is_last(u)):
                    dve.wait_ge(stored, u * 32)
                nc.vector.scalar_tensor_tensor(out=x3_of(u), in0=psZ[:, :], scalar=unscale[:, 1:2], in1=x2,
                                               op0=ALU.mult, op1=ALU.add).then_inc(x_ready[2], 1)

            def make_out(u):
                dve.wait_ge(l3_done, u + 1)
                dve.wait_ge(unscale_ready[2], u + 1)
                nc.vector.scalar_tensor_tensor(out=x3_of(u), in0=psY[:, :], scalar=unscale_of(2, u), in1=x3_of(u),
                                               op0=ALU.mult, op1=ALU.add).then_inc(out_ready, 1)

            def make_low(u):
                dve.wait_ge(la1_done, u + 1)
                nc.vector.scalar_tensor_tensor(
                    out=lowm[:, :, :], in0=psS[:, 0:N1].rearrange("p (l r) -> p r l", l=NL), scalar=c1[:, 0:1],
                    in1=lmask[:, bass.ds(u, 1), :].to_broadcast([P, R1, NL]),
                    op0=ALU.mult, op1=ALU.mult).then_inc(low_masked, 1)
                dve.wait_ge(low_masked, u + 1)
                nc.vector.tensor_reduce(low[:, :], lowm[:, :, :], X, ALU.add).then_inc(low_chain, 1)
                dve.wait_ge(low_chain, u * 2 + 1)
                nc.vector.tensor_copy(lowp[:, 2, :], low[:, :])
                nc.vector.tensor_copy(lowp[:, 0, :], low[:, :]).then_inc(low_chain, 1)
                dve.wait_ge(low_chain, u * 2 + 2)
                nc.vector.tensor_tensor(lowp[:, 1, :], low[:, :], lowp[:, 0, :].bitcast(F32), ALU.subtract
                                        ).then_inc(low_ready, 1)

            GLINKS = 11

            def make_gates(u):
                base = u * GLINKS
                nc.vector.tensor_scalar(lbias[:, :], iotae, tok[:, 1, bass.ds(u, 1)], 5.0, ALU.is_equal, ALU.mult
                                        ).then_inc(gate_chain, 1)
                dve.wait_ge(gate_chain, base + 1)
                dve.wait_ge(la3_done, u + 1)
                dve.wait_ge(inv3_ready, u + 1)
                nc.vector.scalar_tensor_tensor(out=logits[:, :], in0=psS[:, P:N3], scalar=inv3[:, 0:1],
                                               in1=lbias[:, :],
                                               op0=ALU.mult, op1=ALU.add).then_inc(gate_chain, 1)
                dve.drain()
                nc.vector.max(top8[:, :], logits[:, :]).then_inc(gate_chain, 1)
                dve.wait_ge(gate_chain, base + 3)
                nc.vector.tensor_scalar(nmax[:, :], top8[:, 0:1], -1.0, None, ALU.mult).then_inc(top_ready, 1)
                nc.vector.max_index(topi[:, :], top8[:, :], logits[:, :]).then_inc(gate_chain, 1)
                dve.wait_ge(gate_chain, base + 4)
                nc.vector.tensor_copy(topf[:, :], topi[:, :]).then_inc(gate_chain, 1)
                dve.wait_ge(exp_ready, u + 1)
                nc.vector.tensor_scalar(g[:, 1:2], g[:, 0:1], 1.0, None, ALU.add).then_inc(gate_chain, 1)
                dve.wait_ge(gate_chain, base + 6)
                nc.vector.reciprocal(g[:, 2:3], g[:, 1:2]).then_inc(gate_chain, 1)
                dve.wait_ge(gate_chain, base + 7)
                nc.vector.tensor_scalar(g[:, 3:4], g[:, 2:3], g[:, 0:1], c3[:, 0:1], ALU.mult, ALU.mult
                                        ).then_inc(gate_chain, 1)
                nc.vector.tensor_scalar(gates[:, 0, :], iotae, topf[:, 0:1], g[:, 2:3], ALU.is_equal, ALU.mult
                                        ).then_inc(gate_chain, 1)
                dve.wait_ge(gate_chain, base + 9)
                nc.vector.tensor_scalar(gates[:, 1, :], iotae, topf[:, 1:2], g[:, 3:4], ALU.is_equal, ALU.mult
                                        ).then_inc(gate_chain, 1)
                dve.wait_ge(gate_chain, base + 10)
                nc.vector.scalar_tensor_tensor(out=gates[:, 0, :], in0=gates[:, 0, :], scalar=c3[:, 0:1],
                                               in1=gates[:, 1, :], op0=ALU.mult, op1=ALU.add
                                               ).then_inc(gate_chain, 1)
                dve.wait_ge(gate_chain, base + 11)
                nc.vector.tensor_tensor(hg[:, :].rearrange("p (e r) -> p e r", e=NE),
                                        psS[:, 0:P].rearrange("p (e r) -> p e r", e=NE),
                                        gates[:, 0, :].unsqueeze(2).to_broadcast([P, NE, RE]),
                                        ALU.mult).then_inc(hg_chain, 1)
                dve.wait_ge(hg_chain, u * 2 + 1)
                nc.vector.tensor_copy(hgp[:, HI, :], hg[:, :]).then_inc(hg_chain, 1)
                dve.wait_ge(hg_chain, u * 2 + 2)
                nc.vector.tensor_tensor(hgp[:, LO, :], hg[:, :], hgp[:, HI, :].bitcast(F32), ALU.subtract
                                        ).then_inc(hg_ready, 1)

            def tile_step(t, last):
                n, prior, slot = new_adapter(dve, t, 0)
                make_x2(t)
                make_gates(t - 1)
                with dve.If(n > 0):
                    adapter_low(prior, slot, True, [NCHUNK - 1])
                second_adapter(t, True)
                if last:
                    row_unscale(1, t)
                    make_x3(t, False)
                    make_out(t - 1)
                    return
                make_x1(t + 1)
                tile_end(t)

            def tile_end(t):
                row_unscale(1, t)
                n, prior, slot = new_adapter(dve, t + 1, 0)
                make_out(t - 1)
                with dve.If(n > 0):
                    adapter_scale(prior, slot, True)
                make_x3(t, False)
                make_low(t + 1)
                with dve.If(n > 0):
                    adapter_low(prior, slot, True, range(NCHUNK - 1))

            links = [0]

            def link(ins):
                ins.then_inc(route_chain, 1)
                links[0] += 1
                dve.wait_ge(route_chain, links[0])

            nc.vector.memset(ones[:, :], 1.0)
            nc.vector.memset(winvtop[:, :], 1.0)
            nc.vector.memset(zrow[:, :], 0.0)
            nc.vector.memset(new[:, 0:1], 1.0)
            nc.vector.memset(ctlf[:, :, :], 0.0)
            link(nc.vector.memset(w0[:, :], 0.0))
            dve.wait_ge(ids_loaded, 16 * 5)
            nc.vector.tensor_copy(identh[:, :], ident)
            nc.vector.tensor_copy(vals[:, 0:1], iotac)
            nc.vector.tensor_copy(vals[:, 1:4], idcol[:, :])
            link(nc.vector.tensor_copy(idrowf[:, :], idrow[:, :]))
            nc.vector.scalar_tensor_tensor(out=keyrow[:, :], in0=idrowf[:, :], scalar=float(B), in1=iotar,
                                           op0=ALU.mult, op1=ALU.add)
            link(nc.vector.scalar_tensor_tensor(out=keycol[:, :], in0=vals[:, 1:2], scalar=float(B), in1=iotac,
                                                op0=ALU.mult, op1=ALU.add))
            link(nc.vector.tensor_scalar(before[:, :], keyrow[:, :], keycol[:, 0:1], None, ALU.is_lt))
            link(nc.vector.tensor_reduce(pos[:, :], before[:, :], X, ALU.add))
            nc.vector.tensor_scalar(perm1h[:, :], iotar, pos[:, 0:1], None, ALU.is_equal).then_inc(keys_ready, 1)
            dve.wait_ge(sorted_done, 1)
            link(nc.vector.tensor_copy(srt[:, :, :], psS[0:1, 0:4 * B].rearrange("p (n b) -> p n b", n=4)))
            nc.vector.tensor_copy(batch[:, :], srt[:, 0, :])
            nc.vector.tensor_copy(w0id[:, :], srt[:, 1, :])
            link(nc.vector.tensor_tensor(new[:, 1:B], srt[:, 1, 1:B], srt[:, 1, 0:B - 1], ALU.not_equal))
            nc.vector.tensor_tensor_scan(rank[:, :], new[:, :], zrow[:, :], 0.0, ALU.add, ALU.add)
            nc.vector.tensor_tensor_scan(parity[:, :], new[:, :], zrow[:, :], 1.0, ALU.not_equal, ALU.add
                                         ).then_inc(route_chain, 1)
            links[0] += 1
            dve.wait_ge(route_chain, links[0])

            def pair(row, h):
                return row.rearrange("p (t h) -> p h t", h=2)[:, h, :]

            def ctl_row(n):
                return ctlf[:, n, 0:NT]

            new0, new1 = pair(new[:, :], 0), pair(new[:, :], 1)
            par0, par1 = pair(parity[:, :], 0), pair(parity[:, :], 1)
            ad0, ad1 = pair(srt[:, 1, :], 0), pair(srt[:, 1, :], 1)
            nc.vector.tensor_tensor(ctl_row(N_1), new0, new1, ALU.max)
            nc.vector.tensor_tensor(ctl_row(N_2), new0, new1, ALU.mult)
            nc.vector.tensor_scalar(ctl_row(R_2), pair(rank[:, :], 1), -1.0, None, ALU.add)
            nc.vector.tensor_copy(ctl_row(AD_2), ad1)
            nc.vector.tensor_copy(ctl_row(SL_2), par1)
            nc.vector.scalar_tensor_tensor(out=ctl_row(VARIANT), in0=new1, scalar=2.0, in1=par0,
                                           op0=ALU.mult, op1=ALU.add)
            link(nc.vector.tensor_tensor(ctl_row(AD_1), ad0, ad1, ALU.subtract))
            nc.vector.tensor_tensor(ctl_row(R_1), ctl_row(R_2), ctl_row(N_2), ALU.subtract)
            nc.vector.tensor_tensor(ctl_row(SL_1), ctl_row(SL_2), ctl_row(N_2), ALU.not_equal)
            link(nc.vector.tensor_tensor(ctl_row(AD_1), ctl_row(AD_1), ctl_row(N_2), ALU.mult))
            link(nc.vector.tensor_tensor(ctl_row(AD_1), ctl_row(AD_1), ctl_row(AD_2), ALU.add))
            nc.vector.tensor_copy(ctl[:, :, :], ctlf[:, :, :]).then_inc(ctl_ready, 1)
            dve.wait_ge(tok_done, 1)
            link(nc.vector.tensor_copy(tok[:, :, :], psU[:, 0:3 * NT].rearrange("p (n t) -> p n t", n=3)))
            nc.vector.tensor_scalar(notslot[:, :], tok[:, 2, :], -1.0, 1.0, ALU.mult, ALU.add)
            for n in range(NL):
                nc.vector.tensor_scalar(lmask[:, :, n], tok[:, 0, :], float(n), 0.5, ALU.is_equal, ALU.mult)
            link(nc.vector.memset(lbias[:, :], 0.0))

            def bound_last_chunk(src, loaded, column, count):
                c = NCHUNK - 1
                dve.wait_ge(*loaded)
                nc.vector.tensor_reduce(partmax[:, column + c:column + c + 1], src[:, c * WCHUNK:WN],
                                        X, ALU.max, apply_absolute_value=True).then_inc(chunkmax_ready, 1)
                dve.wait_ge(chunkmax_ready, count)

            def fixed_low(i, src, n, dst, col, hi_done, before, lo_done):
                low_parts(i, src, lambda c, m: dst[:, HI, c:m], lambda c, m: dst[:, LO, c:m], n,
                          wscale[:, col:col + 1], hi_done, before, lo_done, range(-(-n // WCHUNK)))

            def low_w3(prior, chunks):
                low_parts(at_w3(prior), raw, lambda c, m: w3[:, HI, c:m], lambda c, m: w3[:, LO, c:m], WN,
                          wscale[:, W3_:W3_ + 1], fixed_hi, SMALL_CHUNKS, fixed_lo, chunks)

            def prepare_b1():
                dve.wait_ge(b1_loaded, 16 * 3)
                link(nc.vector.tensor_copy(b1[:, :], b1raw))
                low_rows = slice(2 * R1, 3 * R1)
                nc.vector.tensor_tensor(b1[low_rows, :], b1raw[low_rows, :], b1[low_rows, :].bitcast(F32),
                                        ALU.subtract).then_inc(b1_ready, 1)

            def prepare_b3():
                dve.wait_ge(b3_loaded, 16)
                link(nc.vector.tensor_copy(b3[:, HI, :], b3raw))
                nc.vector.tensor_tensor(b3[:, LO, :], b3raw, b3[:, HI, :].bitcast(F32),
                                        ALU.subtract).then_inc(b3_ready, 1)

            weight_scale(AT_A1, A1_, FROM_A1, 1)
            weight_scale(AT_A3, A3_, FROM_A3, 1)
            fixed_low(AT_A1, a1raw, K * N1, a1, A1_, fixed_hi, 0, fixed_lo)
            fixed_low(AT_A3, a3raw, K * N3, a3, A3_, fixed_hi, 1, fixed_lo)
            dve.wait_ge(fixed_lo, SMALL_CHUNKS)
            dve.wait_ge(l0_done, 1)
            nc.vector.tensor_tensor(x1, psZ[:, :], xin, ALU.add).then_inc(x_ready[0], 1)
            split_scale(0, 0)
            bound_last_chunk(w1raw, (w1_loaded[NCHUNK - 1], 16), FROM_W1, 1)
            weight_max(AT_W1, FROM_W1)
            split_low(0, 0)
            weight_scale_end(AT_W1, W1_)
            prepare_b1()
            fixed_low(AT_W1, w1raw, WN, w1, W1_, whi_ready, 0, wlo_ready)
            row_unscale(0, 0)
            link(nc.vector.tensor_tensor(c1[:, :], wscale[:, W1_:W1_ + 1], winv[:, A1_:A1_ + 1], ALU.mult))
            make_low(0)

            bound_last_chunk(raw, raw_chunks(0)[NCHUNK - 1], FROM_E, 2)
            dve.wait_ge(wlo_ready, NCHUNK)
            weight_scale(AT_E, SLOT, FROM_E)
            make_x2(0)
            make_x1(1)
            adapter_low(0, 0, False, range(NCHUNK))
            second_adapter(0, False)
            row_unscale(1, 0)
            prepare_b3()
            add_x3(0, True)
            split_scale(2, 0)

            third = dve.value_load(ctl[0:1, R_2, 0:1], min_val=0, max_val=1) + 1
            weight_scale(at_w3(third), W3_)
            split_low(2, 0)
            dve.wait_ge(wprep_chain, at_w3(third) * WLINKS + WLINKS)
            row_unscale(2, 0)
            make_low(1)
            low_w3(third, range(NCHUNK))

            n, prior, slot = new_adapter(dve, 1, 0)
            make_x2(1)
            link(nc.vector.tensor_scalar(c3[:, :], wscale[:, W3_:W3_ + 1], winv[:, A3_:A3_ + 1], 2.0,
                                         ALU.mult, ALU.mult))
            make_gates(0)
            with dve.If(n > 0):
                adapter_scale(prior, slot, True)
            make_x1(2)
            with dve.If(n > 0):
                adapter_low(prior, slot, True, range(NCHUNK))
            second_adapter(1, True)
            tile_end(1)

            with dve.Fori(2, NT - 1) as t:
                tile_step(t, False)
            tile_step(NT - 1, True)
            make_gates(NT - 1)
            make_out(NT - 1)

        @block.tensor
        def _(pe):
            def layer0(u, tiles_before):
                pe.wait_ge(x_loaded, (u + 1) * 32)
                pe.wait_ge(w0_loaded, (u + 1) * 32)
                if tiles_before == 1:
                    pe.wait_ge(x_ready[0], 1)
                elif tiles_before == 2:
                    pe.wait_ge(x_ready[2], u - 1)
                for n in range(HALVES):
                    cols = slice(n * BANK, n * BANK + BANK)
                    last = nc.tensor.matmul(psZ[:, cols], w0[:, :], xin[:, cols], start=True, stop=True)
                last.then_inc(l0_done, 1)

            def transposes(n, u, free):
                pe.wait_ge(hi_ready[n], u + 1)
                pe.wait_ge(lo_ready[n], u + 1)
                if free is not None:
                    pe.wait_ge(*free)
                for part in (HI, LO):
                    for k in range(K):
                        last = nc.tensor.transpose(psT[:, part, k, :], parts[:, part, k * P:k * P + P], identh[:, :])
                last.then_inc(xT_done[n], 1)

            def projection(xt, w, n, done):
                for k in range(K):
                    for i, (xp, wp) in enumerate(PASSES):
                        last = nc.tensor.matmul(psS[:, 0:n], xt[:, xp, k, :], w[:, wp, k * n:k * n + n],
                                                start=(k == 0 and i == 0), stop=(k == K - 1 and i == 2))
                last.then_inc(done, 1)

            def product(xt, w, n, blocks):
                for k in blocks:
                    for i, (xp, wp) in enumerate(PASSES):
                        nc.tensor.matmul(psY[:, n * BANK:n * BANK + BANK], xt[:, xp, k, :],
                                         w[:, wp, k * D + n * BANK:k * D + n * BANK + BANK],
                                         start=(k == 0 and i == 0), stop=False)

            CHUNK_BLOCKS = WCHUNK // D

            def blocks_of(c):
                return range(c * CHUNK_BLOCKS, c * CHUNK_BLOCKS + CHUNK_BLOCKS)

            BEFORE, AFTER = range(K - 2), range(K - 2, K)

            def low_rank(n, terms, done):
                for i, (lhsT, b) in enumerate(terms):
                    last = nc.tensor.matmul(psY[:, n * BANK:n * BANK + BANK], lhsT, b[:, n * BANK:n * BANK + BANK],
                                            start=False, stop=(i == len(terms) - 1))
                if n == HALVES - 1:
                    last.then_inc(done, 1)

            def low_transpose(t):
                pe.wait_ge(low_ready, t + 1)
                nc.tensor.transpose(psU[0:3 * R1, 0:P], lowp[:, :, :].rearrange("p a r -> p (a r)").bitcast(F32), ident
                                    ).then_inc(lowT_done, 1)

            def low_rank1(t):
                pe.wait_ge(lowT_copied, t + 1)
                for n in range(HALVES):
                    low_rank(n, [(lowT[:, :], b1)], l1_done)

            def layer1(t, tiles_before):
                pe.wait_ge(xT_copied[0], t + 1)
                if tiles_before == 2:
                    pe.wait_ge(hg_ready, t - 1)
                projection(xT[0], a1, N1, la1_done)
                if tiles_before == 2:
                    pe.wait_ge(out_ready, t - 1)
                product(xT[0], w1, 0, range(K))
                transposes(2, t - 1, (xT_copied[0], t + 1))
                product(xT[0], w1, 1, BEFORE)
                if tiles_before == 2:
                    pe.wait_ge(hgT_copied, t - 1)
                low_transpose(t)
                product(xT[0], w1, 1, AFTER)
                low_rank1(t)

            def projection3(v, x2_next=True):
                pe.wait_ge(xT_copied[2], v + 1)
                if x2_next:
                    pe.wait_ge(low_ready, v + 2)
                projection(xT[2], a3, N3, la3_done)

            def gated_transposes(v, x2_next=True):
                pe.wait_ge(hg_ready, v + 1)
                if x2_next:
                    pe.wait_ge(lowT_copied, v + 2)
                for part in (HI, LO):
                    last = nc.tensor.transpose(psU[:, part * P:part * P + P], hgp[:, part, :].bitcast(F32), ident)
                last.then_inc(hgT_done, 1)

            def low_rank3(v, n):
                pe.wait_ge(hgT_copied, v + 1)
                low_rank(n, [(hgT[:, xp, :], b3[:, wp, :]) for xp, wp in PASSES], l3_done)

            def layer3(v, first):
                projection3(v)
                layer0(v + 2, 2)
                pe.wait_ge(x_ready[1], v + 2)
                for c in range(NCHUNK):
                    if first:
                        pe.wait_ge(fixed_hi, SMALL_CHUNKS + c + 1)
                        pe.wait_ge(fixed_lo, SMALL_CHUNKS + c + 1)
                    product(xT[2], w3, 0, blocks_of(c))
                transposes(1, v + 1, (xT_copied[2], v + 1))
                product(xT[2], w3, 1, BEFORE)
                gated_transposes(v)
                product(xT[2], w3, 1, AFTER)
                if first:
                    pe.wait_ge(b3_ready, 1)
                for n in range(HALVES):
                    low_rank3(v, n)

            def weights2(slot, part, k, n):
                at = (slot * 2 + part) * WN + k * D + n * BANK
                return w2[:, at:at + BANK]

            def layer2_half(variant, n):
                for v in range(4):
                    with pe.If(variant == v):
                        for k in range(K):
                            for i, (xp, wp) in enumerate(PASSES):
                                start, stop = k == 0 and i == 0, k == K - 1 and i == 2
                                cols = slice(n * BANK, n * BANK + BANK)
                                if v < 2:
                                    last = nc.tensor.matmul(psZ[:, cols], xT[1][:, xp, k, :], weights2(v, wp, k, n),
                                                            start=start, stop=stop)
                                else:
                                    for h, slot in enumerate((v - 2, 3 - v)):
                                        rows = slice(h * C, h * C + C)
                                        last = nc.tensor.matmul(psZ[rows, cols], xT[1][:, xp, k, rows],
                                                                weights2(slot, wp, k, n), start=start, stop=stop)
                        if n == HALVES - 1:
                            last.then_inc(l2_done, 1)

            def layer2_blocks(t0_slots, n, blocks):
                cols = slice(n * BANK, n * BANK + BANK)
                for k in blocks:
                    for i, (xp, wp) in enumerate(PASSES):
                        start, stop = k == 0 and i == 0, k == K - 1 and i == 2
                        if len(t0_slots) == 1:
                            last = nc.tensor.matmul(psZ[:, cols], xT[1][:, xp, k, :],
                                                    weights2(t0_slots[0], wp, k, n), start=start, stop=stop)
                        else:
                            for h, slot in enumerate(t0_slots):
                                rows = slice(h * C, h * C + C)
                                last = nc.tensor.matmul(psZ[rows, cols], xT[1][:, xp, k, rows],
                                                        weights2(slot, wp, k, n), start=start, stop=stop)
                return last

            def layer2_first():
                pe.wait_ge(xT_copied[1], 1)
                pe.wait_ge(x_ready[0], 2)
                variant = pe.value_load(ctl[0:1, VARIANT, 0:1], min_val=0, max_val=3)
                for c in range(NCHUNK):
                    if c == NCHUNK - 1:
                        transposes(0, 1, (xT_copied[1], 1))
                    for v, slots in ((0, [0]), (2, [0, 1])):
                        with pe.If(variant == v):
                            pe.wait_ge(whi_ready, NCHUNK + c + 1)
                            pe.wait_ge(wlo_ready, NCHUNK + c + 1)
                            if v == 2:
                                pe.wait_ge(tile_whi, 1)
                                pe.wait_ge(tile_wlo, 1)
                            for n in range(HALVES):
                                last = layer2_blocks(slots, n, blocks_of(c))
                            if c == NCHUNK - 1:
                                last.then_inc(l2_done, 1)

            def layer2(t, x1_next):
                pe.wait_ge(xT_copied[1], t + 1)
                pe.wait_ge(tile_whi, t + 1)
                pe.wait_ge(tile_wlo, t + 1)
                if x1_next:
                    pe.wait_ge(x_ready[0], t + 2)
                variant = pe.value_load(ctl[0:1, VARIANT, bass.ds(t, 1)], min_val=0, max_val=3)
                layer2_half(variant, 0)
                if x1_next:
                    transposes(0, t + 1, (xT_copied[1], t + 1))
                layer2_half(variant, 1)

            pe.wait_ge(keys_ready, 1)
            for n in range(4):
                last = nc.tensor.matmul(psS[0:1, n * B:n * B + B], vals[:, n:n + 1], perm1h[:, :], start=True, stop=True)
            last.then_inc(sorted_done, 1)
            pe.wait_ge(ctl_ready, 1)
            for n, row in enumerate((srt[:, 2, :], srt[:, 3, :], parity[:, :])):
                for h in range(2):
                    last = nc.tensor.matmul(psU[h * C:h * C + C, n * NT:n * NT + NT], ones[:, 0:C],
                                            row.rearrange("p (t h) -> p h t", h=2)[:, h, :], start=True, stop=True)
            last.then_inc(tok_done, 1)

            layer0(0, 0)
            transposes(0, 0, None)
            pe.wait_ge(fixed_hi, SMALL_CHUNKS)
            pe.wait_ge(fixed_lo, SMALL_CHUNKS)
            pe.wait_ge(xT_copied[0], 1)
            projection(xT[0], a1, N1, la1_done)
            for c in range(NCHUNK):
                pe.wait_ge(whi_ready, c + 1)
                pe.wait_ge(wlo_ready, c + 1)
                for n in range(HALVES):
                    product(xT[0], w1, n, blocks_of(c))
            low_transpose(0)
            pe.wait_ge(b1_ready, 1)
            low_rank1(0)
            layer0(1, 1)
            transposes(1, 0, (xT_copied[0], 1))
            layer2_first()
            layer1(1, 1)
            layer3(0, True)
            layer2(1, True)
            with pe.Fori(2, NT - 1) as t:
                layer1(t, 2)
                layer3(t - 1, False)
                layer2(t, True)
            last_t = NT - 1
            layer1(last_t, 2)
            projection3(last_t - 1)
            pe.wait_ge(x_ready[1], last_t + 1)
            product(xT[2], w3, 0, range(K))
            transposes(1, last_t, (xT_copied[2], last_t))
            gated_transposes(last_t - 1)
            layer2(last_t, False)
            product(xT[2], w3, 1, range(K))
            transposes(2, last_t, (xT_copied[1], last_t + 1))
            for n in range(HALVES):
                low_rank3(last_t - 1, n)
            projection3(last_t, False)
            pe.wait_ge(out_ready, last_t)
            product(xT[2], w3, 0, range(K))
            product(xT[2], w3, 1, BEFORE)
            gated_transposes(last_t, False)
            product(xT[2], w3, 1, AFTER)
            for n in range(HALVES):
                low_rank3(last_t, n)


def kernel(**inputs):
    import concourse.bacc as _bacc
    import numpy as _np
    from concourse import mybir as _mybir
    from concourse.bass_utils import run_bass_kernel_spmd as _run

    x = _np.ascontiguousarray(inputs["x"])
    b, c, d = x.shape
    k = d // 128

    def by_contraction(w):
        return _np.ascontiguousarray(w.reshape(w.shape[0], k, 128).transpose(2, 1, 0))

    def flat(w):
        return w.reshape(128, -1)

    nl, _, r1 = inputs["L1_cond_lora_A"].shape
    ne, r3, _ = inputs["L3_cond_A"].shape
    w2 = inputs["L2_cond_weight"]
    na = w2.shape[0]
    a1 = _np.ascontiguousarray(inputs["L1_cond_lora_A"].reshape(nl, k, 128, r1).transpose(2, 1, 0, 3)).reshape(128, k, nl * r1)
    a3 = by_contraction(_np.concatenate([inputs["L3_cond_A"].reshape(ne * r3, d), inputs["L3_cond_Wr"]], 0))
    consts = _np.zeros((128, 128 + b + 1), _np.float32)
    consts[:, 0:128] = _np.eye(128, dtype=_np.float32)
    consts[:, 128:128 + b] = _np.arange(b, dtype=_np.float32)
    consts[:, 128 + b] = _np.arange(128, dtype=_np.float32)
    arrays = {
        "x": x,
        "itok_adapter": _np.ascontiguousarray(inputs["itok_B_0_15"]),
        "itok_label": _np.ascontiguousarray(inputs["itok_B_0_2"]),
        "itok_language": _np.ascontiguousarray(inputs["itok_B_0_7"]),
        "W0": _np.ascontiguousarray(inputs["L0_cond_weights"]),
        "W1": flat(by_contraction(inputs["L1_cond_W"])),
        "A1": a1,
        "B1": _np.ascontiguousarray(inputs["L1_cond_lora_B_w"].T),
        "W2": _np.ascontiguousarray(w2.reshape(na, d, k, 128).transpose(0, 3, 2, 1)).reshape(na, 128, k * d),
        "W3": flat(by_contraction(inputs["L3_cond_W"])),
        "A3": a3,
        "B3": _np.ascontiguousarray(inputs["L3_cond_B"].transpose(0, 2, 1)).reshape(ne * r3, d),
        "consts": consts,
    }
    nc = _bacc.Bacc("TRN2", target_bir_lowering=False, num_devices=1, dynamic_dma_scratch_size=64)
    ap = {n: nc.dram_tensor(f"in_{n}", a.shape, _mybir.dt.from_np(a.dtype), kind="ExternalInput").ap()
          for n, a in arrays.items()}
    out = nc.dram_tensor("out", x.shape, _mybir.dt.float32, kind="ExternalOutput").ap()
    cond_stack_kernel(nc, ap["x"], [ap["itok_adapter"], ap["itok_label"], ap["itok_language"]], ap["W0"], ap["W1"],
                      ap["A1"], ap["B1"], ap["W2"], ap["W3"], ap["A3"], ap["B3"], ap["consts"], out)
    r = _run(nc, [{f"in_{n}": a for n, a in arrays.items()}], core_ids=[0])
    return r.results[0]["out"]
```
